# Optimizing a Trainium2 kernel written in Bass

```python
import numpy as np
import jax
import jax.numpy as jnp

def _softmax(x, axis=-1):
    return jax.nn.softmax(x, axis=axis)

def _gelu(x):
    return jax.nn.gelu(x, approximate=True)

def _silu(x):
    return jax.nn.silu(x)

def _sigmoid(x):
    return jax.nn.sigmoid(x)

def _layernorm(x, axis=-1, eps=1e-05):
    m = jnp.mean(x, axis=axis, keepdims=True)
    v = jnp.var(x, axis=axis, keepdims=True)
    return (x - m) / jnp.sqrt(v + eps)

def _scatter_add(tgt, idx, src, axis=0):
    return tgt.at[idx].add(src)

def _segment_sum(src, seg, n):
    return jax.ops.segment_sum(src, seg, n)
kernel_name = 'mk_adj_ffn_d1_adj_r2_81d2a6'

def setup_inputs(seed: int=0):
    np.random.seed(seed)
    _w = jnp.asarray

    def _rec_inputs():
        import jax
        import jax.numpy as jnp
        _gk = jax.random.key(seed)
        x = -0.0002928 + 1 * jax.random.normal(jax.random.fold_in(_gk, 1), (2048, 512), jnp.float32)
        _a = jax.random.bernoulli(jax.random.fold_in(_gk, 2), 0.000976562, (2048, 2048))
        _af = _a.astype(jnp.float32)
        adj = _af
        return (x, adj)
    x, adj = _rec_inputs()

    def _L0_gnn_setup():
        import jax, jax.numpy as jnp
        import numpy as np
        import math
        SENT_DIM = 512
        N_SENT = 2048
        key = jax.random.key(seed)
        ks = jax.random.split(key, 8)
        D = SENT_DIM
        s = 1.0 / math.sqrt(D)
        return {'sent_embed': jax.random.normal(ks[0], (N_SENT, D), dtype=jnp.float32), 'adj_tensor': jax.random.randint(ks[1], (N_SENT, N_SENT), 0, 2).astype(jnp.float32), 'W_q': jax.random.uniform(ks[2], (D, D), jnp.float32, -s, s), 'b_q': jax.random.uniform(ks[3], (D,), jnp.float32, -s, s), 'W_k': jax.random.uniform(ks[4], (D, D), jnp.float32, -s, s), 'b_k': jax.random.uniform(ks[5], (D,), jnp.float32, -s, s), 'W_v': jax.random.uniform(ks[6], (D, D), jnp.float32, -s, s), 'b_v': jax.random.uniform(ks[7], (D,), jnp.float32, -s, s)}
    _L0_gnn_all = _L0_gnn_setup()
    _L0_gnn_in = {k: v for k, v in _L0_gnn_all.items() if k in ('W_q', 'b_q', 'W_k', 'b_k', 'W_v', 'b_v')}
    del _L0_gnn_all

    def _L0_ffn_setup():
        import jax, jax.numpy as jnp
        import numpy as np
        B, S, D, E, K, F = (2, 1024, 512, 8, 2, 1024)

        def _swiglu(x, wg, wu, wd):
            return jax.nn.silu(x @ wg) * (x @ wu) @ wd
        key = jax.random.key(seed)
        ks = jax.random.split(key, 9)
        std = 0.02
        return {'X': jax.random.normal(ks[0], (B, S, D), jnp.float32), 'Wr': jax.random.normal(ks[1], (D, E), jnp.float32) * std, 'Wg_s': jax.random.normal(ks[2], (D, F), jnp.float32) * std, 'Wu_s': jax.random.normal(ks[3], (D, F), jnp.float32) * std, 'Wd_s': jax.random.normal(ks[4], (F, D), jnp.float32) * std, 'Wg': jax.random.normal(ks[5], (E, D, F), jnp.float32) * std, 'Wu': jax.random.normal(ks[6], (E, D, F), jnp.float32) * std, 'Wd': jax.random.normal(ks[7], (E, F, D), jnp.float32) * std}
    _L0_ffn_all = _L0_ffn_setup()
    _L0_ffn_in = {k: v for k, v in _L0_ffn_all.items() if k in ('Wr', 'Wg_s', 'Wu_s', 'Wd_s', 'Wg', 'Wu', 'Wd')}
    del _L0_ffn_all
    return {'x': x, 'adj': adj, 'L0_gnn_W_q': _L0_gnn_in['W_q'], 'L0_gnn_b_q': _L0_gnn_in['b_q'], 'L0_gnn_W_k': _L0_gnn_in['W_k'], 'L0_gnn_b_k': _L0_gnn_in['b_k'], 'L0_gnn_W_v': _L0_gnn_in['W_v'], 'L0_gnn_b_v': _L0_gnn_in['b_v'], 'L0_ffn_Wr': _L0_ffn_in['Wr'], 'L0_ffn_Wg_s': _L0_ffn_in['Wg_s'], 'L0_ffn_Wu_s': _L0_ffn_in['Wu_s'], 'L0_ffn_Wd_s': _L0_ffn_in['Wd_s'], 'L0_ffn_Wg': _L0_ffn_in['Wg'], 'L0_ffn_Wu': _L0_ffn_in['Wu'], 'L0_ffn_Wd': _L0_ffn_in['Wd']}

def reference(x, adj, L0_gnn_W_q, L0_gnn_b_q, L0_gnn_W_k, L0_gnn_b_k, L0_gnn_W_v, L0_gnn_b_v, L0_ffn_Wr, L0_ffn_Wg_s, L0_ffn_Wu_s, L0_ffn_Wd_s, L0_ffn_Wg, L0_ffn_Wu, L0_ffn_Wd):
    import jax
    import jax.numpy as jnp

    def _L0_gnn_ref(sent_embed, adj_tensor, W_q, b_q, W_k, b_k, W_v, b_v):
        import jax, jax.numpy as jnp
        import numpy as np
        import math
        SENT_DIM = 512
        N_SENT = 2048
        q = sent_embed @ W_q.T + b_q
        k = sent_embed @ W_k.T + b_k
        v = sent_embed @ W_v.T + b_v
        scale = 1.0 / math.sqrt(sent_embed.shape[-1])
        z = scale * (q @ k.T)
        spare_z = z * adj_tensor
        spare_z = jnp.where(spare_z == 0.0, jnp.asarray(-10000.0, spare_z.dtype), spare_z)
        attn = jax.nn.softmax(spare_z, axis=1)
        out = attn @ v
        return jax.nn.relu(out)

    def _L0_ffn_ref(X, Wr, Wg_s, Wu_s, Wd_s, Wg, Wu, Wd):
        import jax, jax.numpy as jnp
        import numpy as np
        B, S, D, E, K, F = (2, 1024, 512, 8, 2, 1024)

        def _swiglu(x, wg, wu, wd):
            return jax.nn.silu(x @ wg) * (x @ wu) @ wd
        b, s, d = X.shape
        Xf = X.reshape(-1, d)
        T = Xf.shape[0]
        router_w = jax.nn.softmax(Xf @ Wr, axis=-1)
        topk_w, topk_idx = jax.lax.top_k(router_w, K)
        topk_w = jax.nn.softmax(topk_w, axis=-1)
        shared = _swiglu(Xf, Wg_s, Wu_s, Wd_s)
        tok = jnp.arange(T)[:, None]
        w_full = jnp.zeros((T, E), Xf.dtype).at[tok, topk_idx].add(topk_w)
        gate = jax.nn.silu(jnp.einsum('td,edf->etf', Xf, Wg))
        up = jnp.einsum('td,edf->etf', Xf, Wu)
        eout = jnp.einsum('etf,efd->etd', gate * up, Wd)
        specialist = jnp.einsum('etd,te->td', eout, w_full)
        return (shared + specialist).reshape(b, s, d)
    x = x + _L0_gnn_ref(_layernorm(x, axis=-1), adj, L0_gnn_W_q, L0_gnn_b_q, L0_gnn_W_k, L0_gnn_b_k, L0_gnn_W_v, L0_gnn_b_v)
    x = x + _L0_ffn_ref(_layernorm(x, axis=-1)[None], L0_ffn_Wr, L0_ffn_Wg_s, L0_ffn_Wu_s, L0_ffn_Wd_s, L0_ffn_Wg, L0_ffn_Wu, L0_ffn_Wd)[0]
    return x

_drawn_inputs = setup_inputs


def setup_inputs(seed=0):
    import zlib

    import numpy as np

    out = dict(_drawn_inputs(seed))
    spreads = {}
    factors = {'L0_gnn_b_q': 30.586, 'L0_gnn_b_k': 64.0, 'L0_gnn_b_v': 3.156}
    for name, (base, spread) in spreads.items():
        noise = np.random.default_rng([zlib.crc32(name.encode()), seed]).standard_normal(out[name].shape)
        drawn = base * np.exp(spread * noise) if base else spread * noise
        out[name] = jnp.asarray(drawn.astype(out[name].dtype))
    for name, factor in factors.items():
        out[name] = (out[name] * factor).astype(out[name].dtype)
    return out
```

```python
from contextlib import ExitStack

import concourse.bass as bass
from concourse import mybir

F32 = mybir.dt.float32
F32R = mybir.dt.float32r
I32 = mybir.dt.int32
U32 = mybir.dt.uint32
ALU = mybir.AluOpType
ACT = mybir.ActivationFunctionType
AX = mybir.AxisListType.X

P = 128
LN_EPS = 1e-5
MASKED = -10000.0


def gnn_moe(nc, x, adj, w_q, b_q, w_k, b_k, w_v, b_v, w_r, wg_s, wu_s, wd_s, wg, wu, wd, out):
    T, D = x.shape
    E, _, F = wg.shape
    NT = T // P
    DC = D // P
    FC = F // P
    KB = T // 512
    KG = T // 512
    SCALE = 1.0 / float(D) ** 0.5
    STAGES = E + 1
    MAX_TILES = NT + 2 * T // P + E
    SLOT_TILES = MAX_TILES + 2
    ROW = D + 2
    assert D == 512 and F == 1024 and E == 8 and NT == 16

    acc = nc.dram_tensor("acc", [T + P, D], F32, kind="Internal").ap()
    tokens = nc.dram_tensor("tokens", [T, ROW], F32, kind="Internal").ap()
    slots = nc.dram_tensor("slots", [(SLOT_TILES - NT) * P, ROW], F32, kind="Internal").ap()

    with ExitStack() as ctx:
        BASE = 16512

        def at(name, offset, shape, dtype=F32):
            return nc.alloc_sbuf_tensor_at(name, shape, dtype, offset=BASE + offset)

        K = 1024
        ctx.enter_context(nc.sbuf_tensor("arena", [P, 207 * K], mybir.dt.uint8))
        xnT = {"h": at("xnT_h", 0, [P, DC, T], F32R), "l": at("xnT_l", 32 * K, [P, DC, T], F32R)}
        v = {"h": at("v_h", 64 * K, [P, NT, D], F32R), "l": at("v_l", 96 * K, [P, NT, D], F32R)}
        A = {"h": at("A_h", 128 * K, [P, DC, D], F32R), "l": at("A_l", 136 * K, [P, DC, D], F32R)}
        yT = {"h": at("yT_h", 144 * K, [P, DC, 256], F32R), "l": at("yT_l", 148 * K, [P, DC, 256], F32R)}
        pT = {"h": at("pT_h", 152 * K, [P, 2, 512], F32R), "l": at("pT_l", 156 * K, [P, 2, 512], F32R)}
        adj_t = at("adj_t", 160 * K, [P, T])
        sc = at("sc", 168 * K, [P, 2, T])
        fill = at("fill", 184 * K, [P, 512])
        y_f = at("y_f", 186 * K, [P, 2, 256])
        x_t = at("x_t", 188 * K, [P, 2, D])
        x1 = at("x1", 192 * K, [P, D])
        x2T = at("x2T", 194 * K, [P, DC, P])
        x2row = at("x2row", 196 * K, [P, ROW])
        padrow = at("padrow", 198 * K + 64, [P, ROW])
        wk_raw = at("wk_raw", 168 * K, [P, DC, D])
        wq_raw = at("wq_raw", 176 * K, [P, DC, D])
        wv_raw = at("wv_raw", 160 * K, [P, DC, D])
        wq = {"h": at("wq_h", 64 * K, [P, DC, D], F32R), "l": at("wq_l", 72 * K, [P, DC, D], F32R)}
        wk = {"h": at("wk_h", 80 * K, [P, DC, D], F32R), "l": at("wk_l", 88 * K, [P, DC, D], F32R)}
        wvT = {"h": at("wvT_h", 144 * K, [P, DC, D], F32R), "l": at("wvT_l", 152 * K, [P, DC, D], F32R)}
        xn = at("xn", 184 * K, [P, 2, D])
        xT1 = {"h": at("xT1_h", 168 * K, [P, 2, DC, P], F32R), "l": at("xT1_l", 172 * K, [P, 2, DC, P], F32R)}
        v_f = at("v_f", 176 * K, [P, 2, D])
        bk_rep = at("bk_rep", 192 * K, [P, DC, P])
        bv_row = at("bv_row", 196 * K, [P, D])
        gu_h = [[at(f"gu{s}{m}_h", 64 * K * s + 32 * K * m, [P, DC, F], F32R) for m in range(2)] for s in range(2)]
        gu_l = [[at(f"gu{s}{m}_l", 64 * K * s + 32 * K * m + 16 * K, [P, DC, F], F32R) for m in range(2)] for s in range(2)]
        gu_raw = [[at(f"gu{s}{m}_raw", 64 * K * s + 32 * K * m + 16 * K, [P, DC, F]) for m in range(2)] for s in range(2)]
        gate_s_raw = at("gate_s_raw", 128 * K, [P, DC, F])
        dn_h = at("dn_h", 128 * K, [P, FC, D], F32R)
        dn_l = at("dn_l", 144 * K, [P, FC, D], F32R)
        dn_raw = at("dn_raw", 160 * K, [P, FC, D])
        e_x = at("e_x", 176 * K, [P, ROW])
        e_xT = {"h": at("e_xT_h", 179 * K, [P, DC, P], F32R), "l": at("e_xT_l", 181 * K, [P, DC, P], F32R)}
        hid = at("hid", 183 * K, [P, 2, 512])
        sil = at("sil", 187 * K, [P, 2, 512])
        hT = {"h": at("hT_h", 191 * K, [P, FC, P], F32R), "l": at("hT_l", 195 * K, [P, FC, P], F32R)}
        y = at("y", 199 * K, [P, D])
        send = at("send", 64 * K, [P, 4, ROW])
        small = [201 * K + 64]

        def keep(name, shape, dtype=F32):
            n = 4
            for k in shape[1:]:
                n *= k
            t = at(name, small[0], shape, dtype)
            small[0] += -(-n // 32) * 32
            assert small[0] <= 207 * K
            return t

        ident = keep("ident", [P, P])
        before = keep("before", [P, P])
        ones = keep("ones", [P, P])
        w_r_sb = keep("w_r_sb", [P, DC, E])
        bqk = keep("bqk", [P, 2, DC])
        c1 = keep("c1", [P, DC])
        c2 = keep("c2", [P, DC, 2], F32R)
        c2_raw = keep("c2_raw", [P, DC])
        bb = keep("bb", [P, 1])
        s_q = keep("s_q", [P, NT])
        iota8 = keep("iota8", [P, E])
        stat = keep("stat", [P, 6])
        mv = keep("mv", [P, 2, 2])
        var_e = keep("var_e", [P, 2])
        neg_half = keep("neg_half", [P, 1])
        rstd = keep("rstd", [P, 2])
        mx4 = keep("mx4", [P, KB])
        nmx = keep("nmx", [P, 2])
        den = keep("den", [P, 2])
        rden = keep("rden", [P, 1])
        lg = keep("lg", [P, E])
        tok = keep("tok", [P, NT], I32)
        nlm = keep("nlm", [P, 1])
        lex = keep("lex", [P, E])
        lsum = keep("lsum", [P, 1])
        lrs = keep("lrs", [P, 1])
        rw = keep("rw", [P, E])
        top = keep("top", [P, 8])
        topi = keep("topi", [P, 8], U32)
        topf = keep("topf", [P, 2])
        tdiff = keep("tdiff", [P, 1])
        tex = keep("tex", [P, 1])
        tsum = keep("tsum", [P, 1])
        route = keep("route", [P, 2 * E + 4])
        routes = keep("routes", [P, NT, 2 * E + 4])
        both = keep("both", [P, E])
        rank = keep("rank", [P, E])
        base = keep("base", [P, E])
        rsel = keep("rsel", [P, E])
        place = keep("place", [P, NT, E])
        where = keep("where", [P, NT])
        wherek = keep("wherek", [P, NT])
        pos_i = keep("pos_i", [P, 2, NT], I32)
        idx = keep("idx", [P, 4], I32)
        cnt_i = keep("cnt_i", [P, E], I32)
        tiles_i = keep("tiles_i", [P, E], I32)
        tiles_f = keep("tiles_f", [P, E])
        bnd = keep("bnd", [P, E + 2])
        off = keep("off", [P, E])
        cut = keep("cut", [P, 2, E + 1])
        table = keep("table", [P, 32], I32)
        meta_next = keep("meta_next", [P, 2])
        meta = keep("meta", [P, 2])

        bank = [ctx.enter_context(nc.psum_tensor(f"bank{n}", [P, 512], F32)) for n in range(8)]
        sems = {}

        def sem(name):
            if name not in sems:
                sems[name] = ctx.enter_context(nc.semaphore(name))
            return sems[name]

        def wait(eng, name, value):
            if isinstance(value, int) and value <= 0:
                return
            eng.wait_ge(sem(name), value)

        def wait_apart(eng, name, value):
            wait(eng, name, value)
            if not isinstance(value, int):
                eng.sem_inc(sem(f"waits_{eng.engine.name}"), 1)

        def rows(a, t):
            return a[bass.ds(t * P, P), :]

        PASSES = (("h", "h"), ("h", "l"), ("l", "h"))

        def product(pe, o, lhs, rhs, chunks, first=True, last=True):
            n = 0
            for c in chunks:
                for a, b in PASSES:
                    n += 1
                    mm = pe.matmul(o, lhs(a, c), rhs(b, c), start=first and n == 1,
                                   stop=last and n == 3 * len(chunks))
            return mm

        block = ctx.enter_context(nc.Block())

        SPLIT_GU = 2 * DC
        SPLIT_DN = 4
        UNPLACED = 2
        EARLY = 12

        def queries_follow(j, b, nxt):
            return nxt and b == 0 and (not isinstance(j, int) or j + 1 < NT // 2)

        @block.sync
        def _(sp):
            def load_x(t, b):
                sp.dma_start(x_t[:, b, :], rows(x, t)).then_inc(sem(f"x_in{b}"), 16)

            load_x(0, 0)
            load_x(1, 1)
            sp.dma_start(bqk[:, 0, :], b_q.rearrange("(p c) -> p c", c=DC)).then_inc(sem("in_b"), 16)
            sp.dma_start(bqk[:, 1, :], b_k.rearrange("(p c) -> p c", c=DC)).then_inc(sem("in_b"), 16)
            sp.dma_start(wk_raw[:], w_k.rearrange("(p c) n -> p c n", c=DC)).then_inc(sem("in_wk"), 16)
            sp.dma_start(wq_raw[:], w_q.rearrange("(p c) n -> p c n", c=DC)).then_inc(sem("in_wq"), 16)
            sp.dma_start(wv_raw[:], w_v.rearrange("(c p) n -> p c n", p=P)).then_inc(sem("in_wv"), 16)
            sp.dma_start(bv_row[:], b_v.rearrange("(a n) -> a n", a=1).broadcast_to([P, D])).then_inc(sem("in_bv"), 16)
            sp.dma_start(w_r_sb[:], w_r.rearrange("(c p) e -> p c e", p=P)).then_inc(sem("in_wr"), 16)

            with sp.Fori(1, NT // 2) as j:
                for b in range(2):
                    wait(sp, "ln1_done", 2 * j + b - 1)
                    load_x(2 * j + b, b)
            wait(sp, "ln1_done", NT)
            wait(sp, "wv_turned", DC)
            sp.dma_start(adj_t[:], rows(adj, 0)).then_inc(sem("adj_in"), 16)

            def attention_step(i, b, after):
                if not isinstance(i, int) or i < NT - 1:
                    wait(sp, "scored", 4 * i + 4)
                    sp.dma_start(adj_t[:], rows(adj, i + 1)).then_inc(sem("adj_in"), 16)
                if not isinstance(i, int) or i < NT:
                    wait(sp, "x1_done", i - 1)
                    sp.dma_start(x_t[:, b, :], rows(x, i)).then_inc(sem(f"xr_in{b}"), 16)
                if after:
                    wait(sp, "x1_done", i)
                    sp.dma_start(rows(acc, i - 1), x1[:]).then_inc(sem("x1_out"), 16)
                    wait(sp, "x2_done", i)
                    wait(sp, "x2meta", i)
                    sp.dma_start(rows(tokens, i - 1), x2row[:]).then_inc(sem("x2_out"), 16)

            attention_step(0, 0, False)
            attention_step(1, 1, True)
            with sp.Fori(1, NT // 2 - 1) as j:
                attention_step(2 * j, 0, True)
                attention_step(2 * j + 1, 1, True)
            attention_step(NT - 2, 0, True)
            wait(sp, "y_ps", NT)
            sp.dma_start(gate_s_raw[:], wg_s.rearrange("(c p) f -> p c f", p=P)).then_inc(sem("gate_s_in"), 16)
            attention_step(NT - 1, 1, True)
            wait(sp, "scores", 4 * NT)
            sp.dma_start(gu_raw[0][1][:], wu_s.rearrange("(c p) f -> p c f", p=P)).then_inc(sem("gu_in0"), 16)
            wait(sp, "p_turned", 4 * NT)
            sp.dma_start(e_x[:], rows(tokens, 0)).then_inc(sem("e_x_in"), 16)
            attention_step(NT, 0, True)
            wait(sp, "ranked", NT)
            wait(sp, "x1_out", 16 * NT)
            wait(sp, "x2_out", 16 * NT)
            sp.wait_ge(sem("pad_out"), 16 * (SLOT_TILES - NT + 1))
            sp.dma_start(dn_raw[:], wd_s.rearrange("(c p) d -> p c d", p=P)).then_inc(sem("dn_in"), 16)
            def load_send(t, k):
                sp.dma_start(send[:, k, :], rows(tokens, t)).then_inc(sem(f"send_in{k}"), 16)
            for k in range(4):
                load_send(k // 2, k)
            with sp.Fori(1, NT // 2) as j:
                for k in range(4):
                    sp.wait_ge(sem(f"sent{k}"), j * 16)
                    load_send(2 * j + k // 2, k)
            for k in range(4):
                sp.wait_ge(sem(f"sent{k}"), NT // 2 * 16)
            wait(sp, "table", 1)

            def load_gate_up(e, s):
                for m, w in enumerate((wg, wu)):
                    sp.dma_start(gu_raw[s][m][:], w[bass.ds(e, 1), :, :].rearrange("e (c p) f -> p (e c) f", p=P)).then_inc(sem(f"gu_in{s}"), 16)

            def load_down(e):
                wait(sp, "dn_l", SPLIT_DN * (e + 1))
                sp.dma_start(dn_raw[:], wd[bass.ds(e, 1), :, :].rearrange("e (c p) d -> p (e c) d", p=P)).then_inc(sem("dn_in"), 16)

            load_gate_up(0, 1)
            load_down(0)
            wait(sp, "up_done", NT)
            load_gate_up(1, 0)
            load_down(1)
            with sp.Fori(1, E // 2) as j:
                for s in range(2):
                    e = 2 * j + s
                    end = sp.value_load(table[0:1, bass.ds(e, 1)], min_val=NT, max_val=MAX_TILES)
                    wait(sp, "up_done", end)
                    load_gate_up(e, 1 - s)
                    load_down(e)
            n_tiles = sp.value_load(table[0:1, E + 1:E + 2], min_val=NT, max_val=MAX_TILES)
            wait(sp, "e_x_in", n_tiles * 16 + 32)
            wait(sp, "added", n_tiles * 16)
            half = T // 2
            sp.dma_start(out[0:half, :], acc[0:half, :]).then_inc(sem("out"), 16)
            sp.dma_start(out[half:T, :], acc[half:T, :]).then_inc(sem("out"), 16)
            sp.wait_ge(sem("out"), 32)

        @block.gpsimd
        def _(pool):
            pool.memset(ident[:], 0.0).then_inc(sem("pz"), 1)
            pool.memset(before[:], 1.0).then_inc(sem("pz"), 1)
            pool.memset(ones[:], 1.0).then_inc(sem("consts"), 1)
            pool.memset(neg_half[:], -0.5).then_inc(sem("consts"), 1)
            pool.memset(base[:], 0.0).then_inc(sem("consts"), 1)
            pool.iota(iota8[:], pattern=[[1, E]], base=0, channel_multiplier=0,
                      allow_small_or_imprecise_dtypes=True).then_inc(sem("consts"), 1)
            pool.iota(tok[:], pattern=[[P, NT]], base=0, channel_multiplier=1).then_inc(sem("tok"), 1)
            pool.wait_ge(sem("pz"), 2)
            pool.affine_select(out=ident[:], in_=ident[:], compare_op=ALU.not_equal, fill=1.0, base=0,
                               pattern=[[-1, P]], channel_multiplier=1).then_inc(sem("consts"), 1)
            pool.affine_select(out=before[:], in_=before[:], compare_op=ALU.is_gt, fill=0.0, base=0,
                               pattern=[[1, P]], channel_multiplier=-1).then_inc(sem("consts"), 1)
            pool.memset(padrow[:, 0:D + 1], 0.0).then_inc(sem("pad"), 1)
            pool.iota(padrow[:, D + 1:ROW].bitcast(I32), pattern=[[0, 1]], base=T, channel_multiplier=1).then_inc(sem("pad"), 1)

            def power(n, b):
                wait(pool, "var", n)
                pool.tensor_tensor(rstd[:, b:b + 1], var_e[:, b:b + 1], neg_half[:], ALU.pow).then_inc(sem("rstd"), 1)

            pool.wait_ge(sem("consts"), 6)
            power(1, 0)
            power(2, 1)
            with pool.Fori(0, NT // 2 - 1) as j:
                for b in range(2):
                    t = 2 * j + b
                    pool.wait_ge(sem("xT1_l"), t + 1)
                    pool.tensor_copy(xnT["l"][:, :, bass.ds(t * P, P)],
                                     xT1["l"][:, b, :, :].bitcast(F32)).then_inc(sem("xnT_l"), 1)
                    power(t + 3, b)
            for t in range(NT - 2, NT):
                for b in [t % 2]:
                    pool.wait_ge(sem("xT1_l"), t + 1)
                    pool.tensor_copy(xnT["l"][:, :, bass.ds(t * P, P)],
                                     xT1["l"][:, b, :, :].bitcast(F32)).then_inc(sem("xnT_l"), 1)
            pool.wait_ge(sem("pad"), 2)
            pool.dma_start(acc[T:T + P, :], padrow[:, 0:D]).then_inc(sem("pad_out"), 16)
            with pool.Fori(0, SLOT_TILES - NT) as t:
                pool.dma_start(rows(slots, t), padrow[:]).then_inc(sem("pad_out"), 16)
            pool.wait_ge(sem("tok"), 1)
            pool.memset(x2row[:, D:D + 1], 1.0).then_inc(sem("x2_weight"), 1)

            def label(t, b):
                wait(pool, "x2_out", t * 16)
                pool.tensor_copy(x2row[:, D + 1:ROW].bitcast(I32), tok[:, bass.ds(t, 1)]).then_inc(sem("x2meta"), 1)
                power(NT + t + 1, b)

            label(0, 0)
            label(1, 1)
            with pool.Fori(1, NT // 2) as j:
                label(2 * j, 0)
                label(2 * j + 1, 1)

            def add(g):
                wait_apart(pool, "y_done", g + 1)
                pool.indirect_dma_start(acc, bass.IndirectOffsetOnAxis(ap=meta[:, 1:2].bitcast(I32), axis=0),
                                        y[:], None, compute_op=ALU.add).then_inc(sem("added"), 16)
                pool.wait_ge(sem("added"), g * 16 + 16)

            pool.wait_ge(sem("pad_out"), 16 * (SLOT_TILES - NT + 1))
            with pool.Fori(0, UNPLACED) as g:
                add(g)
            pool.wait_ge(sem("table"), 1)
            with pool.Fori(0, NT // 2) as j:
                add(j + UNPLACED)
                for k in range(4):
                    n = 4 * j + k
                    t = 2 * j + k // 2
                    pool.wait_ge(sem(f"send_in{k}"), j * 16 + 16)
                    pool.tensor_copy(send[:, k, D:D + 1], routes[:, bass.ds(t, 1), 2 * E + 2 + k % 2]).then_inc(sem("addressed"), 1)
                    pool.tensor_copy(idx[:, k:k + 1], pos_i[:, k % 2, bass.ds(t, 1)]).then_inc(sem("addressed"), 1)
                    wait_apart(pool, "addressed", 2 * n + 2)
                    pool.indirect_dma_start(slots, bass.IndirectOffsetOnAxis(ap=idx[:, k:k + 1], axis=0),
                                            send[:, k, :], None).then_inc(sem(f"sent{k}"), 16)
            n_tiles = pool.value_load(table[0:1, E + 1:E + 2], min_val=NT, max_val=MAX_TILES)
            with pool.Fori(NT // 2 + UNPLACED, n_tiles) as g:
                add(g)

        @block.tensor
        def _(pe):
            pe.wait_ge(sem("consts"), 6)
            pe.wait_ge(sem("in_wv"), 16)
            for c in range(DC):
                for o in range(DC):
                    mm = pe.transpose(bank[c][:, o * P:(o + 1) * P], wv_raw[:, o, c * P:(c + 1) * P], ident[:])
                mm.then_inc(sem("wv_turned"), 1)
            pe.wait_ge(sem("in_b"), 32)
            pe.wait_ge(sem("in_wk"), 16)
            pe.wait_ge(sem("in_wq"), 16)
            pe.wait_ge(sem("bk_rep"), DC)
            for c in range(2 * DC + 1):
                for o in range(DC):
                    lhs = (wk_raw[:, o, c * P:(c + 1) * P] if c < DC else
                           wq_raw[:, o, (c - DC) * P:(c - DC + 1) * P] if c < 2 * DC else bk_rep[:, o, :])
                    mm = pe.matmul(bank[5][:, 2 * c:2 * c + 2], lhs, bqk[:, :, o], start=o == 0, stop=o == DC - 1)
            mm.then_inc(sem("biases"), 1)
            pe.wait_ge(sem("wqk_l"), 2)
            for c in range(DC):
                pe.wait_ge(sem("wvT_l"), c + 1)
                product(pe, bank[c][:], lambda a, o: wq[a][:, o, c * P:(c + 1) * P],
                        lambda b, o: wk[b][:, o, :], range(DC)).then_inc(sem("A_ps"), 1)
            pe.wait_ge(sem("A_done"), DC)
            pe.wait_ge(sem("c2_done"), 2)

            def before_attention(t, b, this, prev):
                if this:
                    wait(pe, "ln1_done", t + 1)
                    wait(pe, "xT1_l", t - 1)
                    for c in range(DC):
                        mm = pe.transpose(bank[b][:, c * P:(c + 1) * P], xn[:, b, c * P:(c + 1) * P], ident[:])
                    mm.then_inc(sem("xn_turned"), 1)
                if prev:
                    wait(pe, "xT1_l", t)
                    wait(pe, "v_f_done", t - 2)
                    product(pe, bank[3 - b][:], lambda a, c: xT1[a][:, 1 - b, c, :],
                            lambda b_, c: wvT[b_][:, c, :], range(DC)).then_inc(sem("v_ps"), 1)
                    wait(pe, "sq_done", t - 2)
                    for n in range(2 * DC):
                        mm = pe.matmul(bank[5 - b][:, 0:2], xT1["hl"[n // DC]][:, 1 - b, n % DC, :],
                                       c2[:, n % DC, :], start=n == 0, stop=n == 2 * DC - 1)
                    mm.then_inc(sem("sq_ps"), 1)

            before_attention(0, 0, True, False)
            before_attention(1, 1, True, True)
            before_attention(2, 0, True, True)
            before_attention(3, 1, True, True)
            with pe.Fori(2, NT // 2) as j:
                before_attention(2 * j, 0, True, True)
                before_attention(2 * j + 1, 1, True, True)
            before_attention(NT, 0, False, True)

            def queries(j, half):
                for c in range(2):
                    m = 2 * half + c
                    mm = product(pe, bank[7][:, c * 256:(c + 1) * 256], lambda a, d: A[a][:, d, m * P:(m + 1) * P],
                                 lambda b, d: xnT[b][:, d, bass.ds(j * 256, 256)], range(DC))
                mm.then_inc(sem("y_ps"), 1)

            def scores(i, b, n):
                wait(pe, "scored", 4 * (i - 1) + n + 1)
                product(pe, bank[n][:], lambda a, c: yT[a][:, c, b * P:(b + 1) * P],
                        lambda b_, c: xnT[b_][:, c, n * 512:(n + 1) * 512], range(DC)).then_inc(sem("scores"), 1)

            def turn(i, b, g):
                wait(pe, "exp_done", i + 1)
                wait(pe, "pT_l", 4 * i + g - 1)
                for c in range(4):
                    k = 4 * g + c
                    mm = pe.transpose(bank[4 + g % 2][:, c * P:(c + 1) * P], sc[:, b, k * P:(k + 1) * P], ident[:])
                mm.then_inc(sem("p_turned"), 1)

            def attend(i, g):
                wait(pe, "pT_l", 4 * i + g + 1)
                if g == 0:
                    wait(pe, "relu_done", i)
                product(pe, bank[6][:], lambda a, c: pT[a][:, g % 2, c * P:(c + 1) * P],
                        lambda b, c: v[b][:, 4 * g + c, :], range(4), first=g == 0, last=g == 3
                        ).then_inc(sem("attended"), 1)

            def attention_step(j, b, this=True, nxt=True, prev=True):
                i = 2 * j + b
                if nxt:
                    if b == 1:
                        wait(pe, "yT_l", 2 * j + 4)
                    scores(i + 1, 1 - b, 0)
                    scores(i + 1, 1 - b, 1)
                if this:
                    turn(i, b, 0)
                    turn(i, b, 1)
                if prev:
                    wait(pe, "x2_done", i)
                    wait(pe, "ranked", i - 1)
                    if not this:
                        wait(pe, "e_xT_l", 1)
                    for c in range(DC):
                        mm = pe.transpose(bank[7][:, c * P:(c + 1) * P], x2row[:, c * P:(c + 1) * P], ident[:])
                    mm.then_inc(sem("x2_turned"), 1)
                if nxt:
                    scores(i + 1, 1 - b, 2)
                if prev:
                    wait(pe, "x2T_done", i)
                    for c in range(DC):
                        mm = pe.matmul(bank[7][:, 0:E], x2T[:, c, :], w_r_sb[:, c, :], start=c == 0, stop=c == DC - 1)
                    mm.then_inc(sem("logits"), 1)
                if nxt:
                    scores(i + 1, 1 - b, 3)
                ahead = queries_follow(j, b, nxt)
                if ahead:
                    if prev:
                        wait(pe, "logits_read", i)
                    queries(j + 1, 0)
                if this:
                    attend(i, 0)
                    turn(i, b, 2)
                    attend(i, 1)
                if ahead:
                    wait(pe, "yT_f", 2 * j + 3)
                    queries(j + 1, 1)
                if this:
                    turn(i, b, 3)
                    attend(i, 2)
                    attend(i, 3)
                if prev:
                    wait(pe, "logits_read", i)
                    wait(pe, "picked", i)
                    if ahead:
                        wait(pe, "yT_f", 2 * j + 4)
                    pe.matmul(bank[7][:, 0:E], before[:], both[:], start=True, stop=True)
                    pe.matmul(bank[7][:, E:2 * E], ones[:], both[:], start=True, stop=True).then_inc(sem("counted"), 1)

            def turn_rows(g):
                wait(pe, "e_x_in", g * 16 + 16)
                wait(pe, "e_xT_l", g)
                for c in range(DC):
                    mm = pe.transpose(bank[7][:, c * P:(c + 1) * P], e_x[:, c * P:(c + 1) * P], ident[:])
                mm.then_inc(sem("x_turned"), 1)

            pe.wait_ge(sem("xnT_h"), NT)
            pe.wait_ge(sem("xnT_l"), NT)
            pe.wait_ge(sem("v_l"), NT)
            pe.wait_ge(sem("sq_done"), NT)
            queries(0, 0)
            pe.wait_ge(sem("yT_f"), 1)
            queries(0, 1)
            pe.wait_ge(sem("yT_l"), 2)
            for n in range(KB):
                scores(0, 0, n)
            attention_step(0, 0, prev=False)
            attention_step(0, 1)
            with pe.Fori(1, NT // 2 - 1) as j:
                attention_step(j, 0)
                attention_step(j, 1)
            attention_step(NT // 2 - 1, 0)
            attention_step(NT // 2 - 1, 1, nxt=False)
            wait(pe, "ranked", NT - 1)
            turn_rows(0)
            attention_step(NT // 2, 0, this=False, nxt=False)

            def expert_tile(g, s, downs):
                def project(m, f, read):
                    wait(pe, read, g)
                    n = 2 * f + m
                    return product(pe, bank[n][:], lambda a, c: e_xT[a][:, c, :],
                                   lambda b, c: (gu_h if b == "h" else gu_l)[s][m][:, c, f * 512:(f + 1) * 512], range(DC))

                def turn_hidden(f):
                    wait(pe, f"hid{f}", g + 1)
                    wait(pe, f"hT_l{f}", g)
                    for c in range(4):
                        mm = pe.transpose(bank[4 + f][:, c * P:(c + 1) * P], hid[:, f, c * P:(c + 1) * P], ident[:])
                    mm.then_inc(sem(f"h_turned{f}"), 1)

                def down(chunks):
                    return product(pe, bank[6][:], lambda a, c: hT[a][:, c, :],
                                   lambda b, c: (dn_h if b == "h" else dn_l)[:, c, :], chunks,
                                   first=chunks[0] == 0, last=chunks[-1] == FC - 1)

                wait(pe, "e_xT_l", g + 1)
                project(0, 0, "silu0").then_inc(sem("gate0"), 1)
                project(1, 0, "hid0").then_inc(sem("up0"), 1)
                project(0, 1, "silu1").then_inc(sem("gate1"), 1)
                turn_hidden(0)
                project(1, 1, "hid1").then_inc(sem("up_done"), 1)
                wait(pe, "hT_l0", g + 1)
                wait(pe, "y_done", g)
                wait(pe, "dn_l", downs)
                down(range(0, 2))
                turn_hidden(1)
                down(range(2, 4))
                turn_rows(g + 1)
                wait(pe, "hT_l1", g + 1)
                down(range(4, FC)).then_inc(sem("down_done"), 1)

            pe.wait_ge(sem("gu_l"), SPLIT_GU)
            expert_tile(0, 0, SPLIT_DN)
            with pe.Fori(1, NT) as g:
                expert_tile(g, 0, SPLIT_DN)
            pe.wait_ge(sem("table"), 1)
            with pe.Fori(0, E // 2) as j:
                for k in range(2):
                    e = 2 * j + k
                    first = pe.value_load(table[0:1, bass.ds(e + 1, 1)], min_val=NT, max_val=MAX_TILES)
                    end = pe.value_load(table[0:1, bass.ds(e + 2, 1)], min_val=NT, max_val=MAX_TILES)
                    wait_apart(pe, "gu_l", e * SPLIT_GU + 2 * SPLIT_GU)
                    with pe.Fori(first, end) as g:
                        expert_tile(g, 1 - k, e * SPLIT_DN + 2 * SPLIT_DN)

        @block.scalar
        def _(act):
            def copy(o, i, scale=None):
                return act.activation(o, i, ACT.Copy) if scale is None else act.activation(o, i, ACT.Copy, scale=scale)

            act.wait_ge(sem("in_wk"), 16)
            copy(wk["h"][:], wk_raw[:]).then_inc(sem("wqk_h"), 1)
            act.wait_ge(sem("in_wq"), 16)
            copy(wq["h"][:], wq_raw[:]).then_inc(sem("wqk_h"), 1)
            for c in range(DC):
                wait(act, "wv_turned", c + 1)
                copy(wvT["h"][:, c, :], bank[c][:]).then_inc(sem("wvT_h"), 1)
            for c in range(DC):
                wait(act, "A_ps", c + 1)
                copy(A["h"][:, c, :], bank[c][:]).then_inc(sem("A_h"), 1)

            act.wait_ge(sem("biases"), 1)
            act.wait_ge(sem("wqk_l"), 2)

            def before_attention(t, b, this, prev):
                if this:
                    wait(act, "xn_turned", t + 1)
                    wait(act, "sq_ps", t - 1)
                    wait(act, "xnT_h", t - 1)
                    wait(act, "xT1_l", t - 1)
                    copy(xT1["h"][:, b, :, :], bank[b][:].rearrange("p (c q) -> p c q", c=DC)).then_inc(sem("xT1_h"), 1)
                    wait(act, "xT1_h", t + 1)
                    copy(xnT["h"][:, :, bass.ds(t * P, P)], xT1["h"][:, b, :, :].bitcast(F32)).then_inc(sem("xnT_h"), 1)
                if prev:
                    wait(act, "v_f_done", t)
                    copy(v["h"][:, bass.ds(t - 1, 1), :], v_f[:, 1 - b:2 - b, :]).then_inc(sem("v_h"), 1)

            before_attention(0, 0, True, False)
            before_attention(1, 1, True, True)
            before_attention(2, 0, True, True)
            before_attention(3, 1, True, True)
            with act.Fori(2, NT // 2) as j:
                before_attention(2 * j, 0, True, True)
                before_attention(2 * j + 1, 1, True, True)
            before_attention(NT, 0, False, True)

            def pieces(g, split, n, m):
                if split is None:
                    return
                when, s, filling = split
                if when is not None:
                    with act.If(g == when):
                        pieces(g, (None, s, filling), n, m)
                    return
                shared = isinstance(filling, int) and filling == 0
                if n == 0 and shared:
                    wait(act, "gate_s_in", 16)
                    wait(act, "scores", 4 * NT)
                else:
                    wait(act, f"gu_in{s}", filling * 32 + (16 if s == 0 else 0))
                for k in range(n, m):
                    raw = gate_s_raw if shared and k < DC else gu_raw[s][k // DC]
                    copy(gu_h[s][k // DC][:, k % DC, :], raw[:, k % DC, :]).then_inc(sem("gu_h"), 1)

            def turned_rows(g):
                wait(act, "x_turned", g + 1)
                wait(act, "up_done", g)
                wait(act, "e_xT_l", g)
                copy(e_xT["h"][:], bank[7][:].rearrange("p (c q) -> p c q", c=DC)).then_inc(sem("e_xT_h"), 1)

            def queries(n, half):
                wait(act, "yT_f", n + 1)
                copy(yT["h"][:, 2 * half:2 * half + 2, :], y_f[:]).then_inc(sem("yT_h"), 1)

            def probabilities(i, b):
                wait(act, "nmx_done", i + 1)
                act.activation(sc[:, b, :], sc[:, b, :], ACT.Exp, bias=nmx[:, b:b + 1],
                               accum_out=den[:, b:b + 1]).then_inc(sem("exp_done"), 1)

            def group(i, g):
                n = 4 * i + g
                wait(act, "p_turned", n + 1)
                wait(act, "attended", n - 1)
                wait(act, "pT_l", n - 1)
                copy(pT["h"][:, g % 2, :], bank[4 + g % 2][:]).then_inc(sem("pT_h"), 1)

            def attention_step(j, b, this=True, nxt=True, prev=True):
                i = 2 * j + b
                if prev:
                    wait(act, "attended", 4 * i)
                    wait(act, "rden_done", i)
                    wait(act, "x1_out", 16 * (i - 1))
                    wait(act, "x2_done", i - 1)
                    act.activation(x1[:], bank[6][:], ACT.Relu, scale=rden[:, 0:1]).then_inc(sem("relu_done"), 1)
                if this:
                    group(i, 0)
                    group(i, 1)
                if prev:
                    wait(act, "x2_turned", i)
                    wait(act, "logits", i - 1)
                    copy(x2T[:], bank[7][:].rearrange("p (c q) -> p c q", c=DC)).then_inc(sem("x2T_done"), 1)
                    wait(act, "nlm_done", i)
                    act.activation(lex[:], lg[:], ACT.Exp, bias=nlm[:], accum_out=lsum[:]).then_inc(sem("lex_done"), 1)
                ahead = queries_follow(j, b, nxt)
                if ahead:
                    queries(2 * j + 2, 0)
                if prev:
                    wait(act, "tdiff_done", i)
                    act.activation(tex[:], tdiff[:], ACT.Exp).then_inc(sem("tex_done"), 1)
                if this:
                    group(i, 2)
                if ahead:
                    queries(2 * j + 3, 1)
                if this:
                    group(i, 3)
                if nxt:
                    probabilities(i + 1, 1 - b)

            queries(0, 0)
            queries(1, 1)
            probabilities(0, 0)
            attention_step(0, 0, prev=False)
            attention_step(0, 1)
            with act.Fori(1, NT // 2 - 1) as j:
                attention_step(j, 0)
                attention_step(j, 1)
            attention_step(NT // 2 - 1, 0)
            attention_step(NT // 2 - 1, 1, nxt=False)
            pieces(0, (None, 0, 0), 0, DC)
            turned_rows(0)
            wait(act, "meta_next", 1)
            act.dma_start(e_x[:], rows(tokens, 1)).then_inc(sem("e_x_in"), 16)
            attention_step(NT // 2, 0, this=False, nxt=False)

            def split_down(stage, first):
                wait(act, "dn_in", stage * 16 + 16)
                wait(act, "down_done", first)
                for c in range(SPLIT_DN):
                    k = FC // SPLIT_DN
                    copy(dn_h[:, c * k:(c + 1) * k, :], dn_raw[:, c * k:(c + 1) * k, :]).then_inc(sem("dn_h"), 1)

            def expert_tile(g, source, row, split=None):
                for f in range(2):
                    wait(act, f"gate{f}", g + 1)
                    wait(act, f"hid{f}", g)
                    act.activation(sil[:, f, :], bank[2 * f][:], ACT.Silu).then_inc(sem(f"silu{f}"), 1)
                    if f == 0:
                        pieces(g, split, 0, 3)
                for f in range(2):
                    wait(act, f"h_turned{f}", g + 1)
                    wait(act, "down_done", g)
                    wait(act, f"hT_l{f}", g)
                    copy(hT["h"][:, 4 * f:4 * f + 4, :], bank[4 + f][:].rearrange("p (c q) -> p c q", c=4)
                         ).then_inc(sem(f"hT_h{f}"), 1)
                    if f == 0:
                        pieces(g, split, 3, 6)
                turned_rows(g + 1)
                wait(act, "meta_next", g + 2)
                act.dma_start(e_x[:], rows(source, row)).then_inc(sem("e_x_in"), 16)
                wait(act, "down_done", g + 1)
                wait(act, "meta", g + 1)
                wait(act, "added", g * 16)
                copy(y[:], bank[6][:], scale=meta[:, 0:1]).then_inc(sem("y_done"), 1)
                pieces(g, split, 6, SPLIT_GU)

            pieces(0, (None, 0, 0), DC, SPLIT_GU)
            split_down(0, 0)
            expert_tile(0, tokens, 2)
            with act.Fori(1, EARLY) as g:
                expert_tile(g, tokens, g + 2)
            expert_tile(EARLY, tokens, EARLY + 2, (None, 1, 1))
            with act.Fori(EARLY + 1, NT - 2) as g:
                expert_tile(g, tokens, g + 2)
            for k in range(4):
                act.wait_ge(sem(f"sent{k}"), NT // 2 * 16)
            expert_tile(NT - 2, slots, 0)
            expert_tile(NT - 1, slots, 1)
            act.wait_ge(sem("table"), 1)
            with act.Fori(0, E // 2) as j:
                for k in range(2):
                    e = 2 * j + k
                    first = act.value_load(table[0:1, bass.ds(e + 1, 1)], min_val=NT, max_val=MAX_TILES)
                    end = act.value_load(table[0:1, bass.ds(e + 2, 1)], min_val=NT, max_val=MAX_TILES)
                    when = act.value_load(table[0:1, bass.ds(e + 16, 1)], min_val=0, max_val=MAX_TILES)
                    split_down(e + 1, first)
                    with act.Fori(first, end) as g:
                        expert_tile(g, slots, g + 2 - NT, (when, k, j + 1 + k))

        @block.vector
        def _(dve):
            def minus(o, a, b):
                return dve.tensor_tensor(o, a, b.bitcast(F32), ALU.subtract)

            def statistics(a, n, b):
                dve.bn_stats(stat[:], a).then_inc(sem("stat"), 1)
                wait_apart(dve, "stat", n)
                dve.bn_aggr(mv[:, b, :], stat[:]).then_inc(sem("mean_var"), 1)
                wait(dve, "mean_var", n)
                dve.tensor_scalar(var_e[:, b:b + 1], mv[:, b, 1:2], LN_EPS, None, ALU.add).then_inc(sem("var"), 1)

            def normalise(o, a, n, b):
                wait(dve, "rstd", n)
                return dve.tensor_scalar(o, a, mv[:, b, 0:1], rstd[:, b:b + 1], ALU.subtract, ALU.mult)

            def measure(t, b, j):
                dve.wait_ge(sem(f"x_in{b}"), j * 16 + 16)
                wait(dve, "ln1_done", t - 1)
                statistics(x_t[:, b, :], t + 1, b)

            def layer_norm(t, b):
                wait(dve, "xn_turned", t - 1)
                normalise(xn[:, b, :], x_t[:, b, :], t + 1, b).then_inc(sem("ln1_done"), 1)

            measure(0, 0, 0)
            measure(1, 1, 0)
            layer_norm(0, 0)
            dve.wait_ge(sem("consts"), 6)
            dve.wait_ge(sem("in_b"), 32)
            for c in range(DC):
                dve.tensor_scalar(bk_rep[:, c, :], ones[:], bqk[:, 1, c:c + 1], None, ALU.mult).then_inc(sem("bk_rep"), 1)
            for n, (w, raw) in enumerate(((wk, wk_raw), (wq, wq_raw))):
                dve.wait_ge(sem("wqk_h"), n + 1)
                minus(w["l"][:], raw[:], w["h"][:]).then_inc(sem("wqk_l"), 1)
            for c in range(DC):
                dve.wait_ge(sem("wvT_h"), c + 1)
                minus(wvT["l"][:, c, :], bank[c][:], wvT["h"][:, c, :]).then_inc(sem("wvT_l"), 1)
            dve.wait_ge(sem("biases"), 1)
            for c in range(DC):
                dve.tensor_copy(c1[:, c:c + 1], bank[5][:, 2 * c:2 * c + 1]).then_inc(sem("c1_done"), 1)
                dve.tensor_copy(c2_raw[:, c:c + 1], bank[5][:, 2 * (DC + c) + 1:2 * (DC + c) + 2]).then_inc(sem("c1_done"), 1)
            dve.tensor_copy(bb[:], bank[5][:, 4 * DC:4 * DC + 1]).then_inc(sem("c1_done"), 1)
            dve.wait_ge(sem("c1_done"), 2 * DC + 1)
            dve.tensor_copy(c2[:, :, 0], c2_raw[:]).then_inc(sem("c2_done"), 1)
            dve.wait_ge(sem("c2_done"), 1)
            minus(c2[:, :, 1], c2_raw[:], c2[:, :, 0]).then_inc(sem("c2_done"), 1)
            for c in range(DC):
                dve.wait_ge(sem("A_h"), c + 1)
                minus(A["l"][:, c, :], bank[c][:], A["h"][:, c, :]).then_inc(sem("A_done"), 1)

            dve.wait_ge(sem("in_bv"), 16)

            def before_attention(t, b, this, prev, j, further=True):
                if this:
                    if further or b == 0:
                        layer_norm(t + 1, 1 - b)
                    wait(dve, "xT1_h", t + 1)
                    wait(dve, "xnT_l", t - 1)
                    wait(dve, "sq_ps", t - 1)
                    minus(xT1["l"][:, b, :, :], bank[b][:].rearrange("p (c q) -> p c q", c=DC),
                          xT1["h"][:, b, :, :]).then_inc(sem("xT1_l"), 1)
                if prev:
                    wait(dve, "v_ps", t)
                    wait(dve, "v_h", t - 2)
                    wait(dve, "v_l", t - 2)
                    dve.tensor_tensor(v_f[:, 1 - b, :], bank[3 - b][:], bv_row[:], ALU.add).then_inc(sem("v_f_done"), 1)
                    wait(dve, "sq_ps", t)
                    wait(dve, "sq_done", t - 1)
                    dve.tensor_reduce(tsum[:], bank[5 - b][:, 0:2], AX, ALU.add).then_inc(sem("sq_sum"), 1)
                    wait(dve, "sq_sum", t)
                    dve.tensor_scalar(s_q[:, bass.ds(t - 1, 1)], tsum[:], bb[:, 0:1], SCALE, ALU.add,
                                      ALU.mult).then_inc(sem("sq_done"), 1)
                    wait(dve, "v_h", t)
                    minus(v["l"][:, bass.ds(t - 1, 1), :], v_f[:, 1 - b:2 - b, :],
                          v["h"][:, bass.ds(t - 1, 1), :]).then_inc(sem("v_l"), 1)
                if further:
                    measure(t + 2, b, j + 1)

            before_attention(0, 0, True, False, 0)
            before_attention(1, 1, True, True, 0)
            before_attention(2, 0, True, True, 1)
            before_attention(3, 1, True, True, 1)
            with dve.Fori(2, NT // 2 - 1) as j:
                before_attention(2 * j, 0, True, True, j)
                before_attention(2 * j + 1, 1, True, True, j)
            before_attention(NT - 2, 0, True, True, NT // 2 - 1, False)
            before_attention(NT - 1, 1, True, True, NT // 2 - 1, False)
            before_attention(NT, 0, False, True, NT // 2, False)

            def pieces(g, split, n, m):
                if split is None:
                    return
                when, s, stage = split
                if when is not None:
                    with dve.If(g == when):
                        pieces(g, (None, s, stage), n, m)
                    return
                for k in range(n, m):
                    wait(dve, "gu_h", stage * SPLIT_GU + k + 1)
                    raw = gate_s_raw if isinstance(stage, int) and stage == 0 and k < DC else gu_raw[s][k // DC]
                    minus(gu_l[s][k // DC][:, k % DC, :], raw[:, k % DC, :],
                          gu_h[s][k // DC][:, k % DC, :]).then_inc(sem("gu_l"), 1)

            def turned_rows(g):
                wait(dve, "e_x_in", g * 16 + 16)
                wait(dve, "meta", g)
                dve.tensor_copy(meta_next[:].bitcast(I32), e_x[:, D:ROW].bitcast(I32)).then_inc(sem("meta_next"), 1)
                wait(dve, "e_xT_h", g + 1)
                minus(e_xT["l"][:], bank[7][:].rearrange("p (c q) -> p c q", c=DC), e_xT["h"][:]).then_inc(sem("e_xT_l"), 1)

            def queries(n, half):
                wait(dve, "y_ps", n + 1)
                wait(dve, "yT_h", n)
                wait(dve, "yT_l", n)
                for c in range(2):
                    m = 2 * half + c
                    ins = dve.tensor_scalar(y_f[:, c, :], bank[7][:, c * 256:(c + 1) * 256], c1[:, m:m + 1], SCALE,
                                            ALU.add, ALU.mult)
                ins.then_inc(sem("yT_f"), 1)
                wait(dve, "yT_h", n + 1)
                minus(yT["l"][:, 2 * half:2 * half + 2, :], y_f[:], yT["h"][:, 2 * half:2 * half + 2, :]).then_inc(sem("yT_l"), 1)

            def mask(i, b, n):
                wait(dve, "scores", 4 * i + n + 1)
                if n == 0:
                    wait(dve, "adj_in", i * 16 + 16)
                    wait(dve, "p_turned", 4 * (i - 1))
                dve.scalar_tensor_tensor(out=sc[:, b, n * 512:(n + 1) * 512], in0=bank[n][:], scalar=s_q[:, bass.ds(i, 1)],
                                         in1=adj_t[:, n * 512:(n + 1) * 512], op0=ALU.add, op1=ALU.mult
                                         ).then_inc(sem("scored"), 1)

            def fill_zeros(i, b, n):
                part = sc[:, b, n * 512:(n + 1) * 512]
                wait(dve, "scored", 4 * i + n + 1)
                wait(dve, "filled", 4 * i + n)
                dve.tensor_scalar(fill[:], part, 0.0, MASKED, ALU.is_equal, ALU.mult).then_inc(sem("zeros"), 1)
                if n == 0:
                    wait(dve, "nmx_done", i)
                wait_apart(dve, "zeros", 4 * i + n + 1)
                dve.tensor_tensor_reduce(out=part, in0=part, in1=fill[:], scale=1.0, scalar=-3.0e38, op0=ALU.add,
                                         op1=ALU.max, accum_out=mx4[:, n:n + 1]).then_inc(sem("filled"), 1)

            def row_max(i, b):
                wait(dve, "filled", 4 * i + 4)
                wait(dve, "exp_done", i - 1)
                dve.tensor_reduce(nmx[:, b:b + 1], mx4[:], AX, ALU.max, negate=True).then_inc(sem("nmx_done"), 1)

            def group(i, g):
                n = 4 * i + g
                wait(dve, "pT_h", n + 1)
                minus(pT["l"][:, g % 2, :], bank[4 + g % 2][:], pT["h"][:, g % 2, :]).then_inc(sem("pT_l"), 1)

            ROUTER = 15

            def attention_step(j, b, this=True, nxt=True, prev=True):
                i = 2 * j + b
                if prev:
                    wait(dve, "exp_done", i)
                    wait(dve, "relu_done", i - 1)
                    dve.reciprocal(rden[:], den[:, 1 - b:2 - b]).then_inc(sem("rden_done"), 1)
                    wait(dve, "relu_done", i)
                    dve.wait_ge(sem(f"xr_in{1 - b}"), (j + b) * 16)
                    dve.tensor_tensor(x1[:], x1[:], x_t[:, 1 - b, :], ALU.add).then_inc(sem("x1_done"), 1)
                    wait(dve, "x1_done", i)
                    statistics(x1[:], NT + i, 1 - b)
                    wait(dve, "x2_out", 16 * (i - 1))
                    wait(dve, "x2_turned", i - 1)
                    normalise(x2row[:, 0:D], x1[:], NT + i, 1 - b).then_inc(sem("x2_done"), 1)
                if nxt:
                    mask(i + 1, 1 - b, 0)
                    mask(i + 1, 1 - b, 1)
                if this:
                    group(i, 0)
                    group(i, 1)
                if nxt:
                    fill_zeros(i + 1, 1 - b, 0)
                    fill_zeros(i + 1, 1 - b, 1)
                    mask(i + 1, 1 - b, 2)
                    fill_zeros(i + 1, 1 - b, 2)
                if prev:
                    wait(dve, "logits", i)
                    dve.tensor_copy(lg[:], bank[7][:, 0:E]).then_inc(sem("logits_read"), 1)
                    wait(dve, "logits_read", i)
                    dve.tensor_reduce(nlm[:], lg[:], AX, ALU.max, negate=True).then_inc(sem("nlm_done"), 1)
                if nxt:
                    mask(i + 1, 1 - b, 3)
                    fill_zeros(i + 1, 1 - b, 3)
                ahead = queries_follow(j, b, nxt)
                if ahead:
                    queries(2 * j + 2, 0)

                at_start = (i - 1) * ROUTER
                steps = [0]

                def then(ins):
                    steps[0] += 1
                    ins.then_inc(sem("routing"), 1)
                    wait_apart(dve, "routing", at_start + steps[0])

                if prev:
                    wait(dve, "lex_done", i)
                    then(dve.reciprocal(lrs[:], lsum[:]))
                    then(dve.tensor_scalar(rw[:], lex[:], lrs[:, 0:1], None, ALU.mult))
                    then(dve.max(top[:], rw[:]))
                    then(dve.max_index(topi[:], top[:], rw[:]))
                    dve.tensor_tensor(tdiff[:], top[:, 1:2], top[:, 0:1], ALU.subtract).then_inc(sem("tdiff_done"), 1)
                    then(dve.tensor_copy(topf[:], topi[:, 0:2]))
                    for k in range(2):
                        then(dve.tensor_scalar(route[:, k * E:(k + 1) * E], iota8[:], topf[:, k:k + 1], None, ALU.is_equal))
                    dve.tensor_tensor(both[:], route[:, 0:E], route[:, E:2 * E], ALU.add).then_inc(sem("picked"), 1)
                if this:
                    group(i, 2)
                if prev:
                    wait(dve, "tex_done", i)
                    then(dve.tensor_scalar(tsum[:], tex[:], 1.0, None, ALU.add))
                    then(dve.reciprocal(route[:, 2 * E + 2:2 * E + 3], tsum[:]))
                    then(dve.tensor_tensor(route[:, 2 * E + 3:2 * E + 4], tex[:], route[:, 2 * E + 2:2 * E + 3], ALU.mult))
                if ahead:
                    queries(2 * j + 3, 1)
                if this:
                    group(i, 3)
                if nxt:
                    row_max(i + 1, 1 - b)
                if prev:
                    wait(dve, "counted", i)
                    then(dve.tensor_tensor(rank[:], bank[7][:, 0:E], base[:], ALU.add))
                    for k in range(2):
                        then(dve.tensor_tensor_reduce(out=rsel[:], in0=route[:, k * E:(k + 1) * E], in1=rank[:], scale=1.0,
                                                      scalar=0.0, op0=ALU.mult, op1=ALU.add,
                                                      accum_out=route[:, 2 * E + k:2 * E + k + 1]))
                    then(dve.tensor_copy(routes[:, bass.ds(i - 1, 1), :], route[:].rearrange("p (a n) -> p a n", a=1)))
                    then(dve.tensor_tensor(base[:], base[:], bank[7][:, E:2 * E], ALU.add))
                    dve.tensor_copy(rsel[:], rank[:]).then_inc(sem("ranked"), 1)
                    assert steps[0] == ROUTER

            queries(0, 0)
            queries(1, 1)
            for n in range(KB):
                mask(0, 0, n)
                fill_zeros(0, 0, n)
            row_max(0, 0)
            attention_step(0, 0, prev=False)
            attention_step(0, 1)
            with dve.Fori(1, NT // 2 - 1) as j:
                attention_step(j, 0)
                attention_step(j, 1)
            attention_step(NT // 2 - 1, 0)
            attention_step(NT // 2 - 1, 1, nxt=False)
            pieces(0, (None, 0, 0), 0, DC)
            turned_rows(0)
            attention_step(NT // 2, 0, this=False, nxt=False)

            def split_down(stage):
                for c in range(SPLIT_DN):
                    k = FC // SPLIT_DN
                    wait(dve, "dn_h", stage * SPLIT_DN + c + 1)
                    minus(dn_l[:, c * k:(c + 1) * k, :], dn_raw[:, c * k:(c + 1) * k, :],
                          dn_h[:, c * k:(c + 1) * k, :]).then_inc(sem("dn_l"), 1)

            def expert_tile(g, split=None):
                for f in range(2):
                    wait(dve, f"silu{f}", g + 1)
                    wait(dve, "up0" if f == 0 else "up_done", g + 1)
                    wait(dve, f"h_turned{f}", g)
                    dve.tensor_tensor(hid[:, f, :], bank[2 * f + 1][:], sil[:, f, :], ALU.mult).then_inc(sem(f"hid{f}"), 1)
                    if f == 0:
                        wait(dve, "added", g * 16)
                        wait(dve, "y_done", g)
                        wait(dve, "meta_next", g + 1)
                        dve.tensor_copy(meta[:].bitcast(I32), meta_next[:].bitcast(I32)).then_inc(sem("meta"), 1)
                        pieces(g, split, 0, 2)
                        hidden(g, 0)
                        pieces(g, split, 2, 3)
                pieces(g, split, 3, 4)
                hidden(g, 1)
                turned_rows(g + 1)
                pieces(g, split, 4, SPLIT_GU)

            def hidden(g, f):
                wait(dve, f"hT_h{f}", g + 1)
                minus(hT["l"][:, 4 * f:4 * f + 4, :], bank[4 + f][:].rearrange("p (c q) -> p c q", c=4),
                      hT["h"][:, 4 * f:4 * f + 4, :]).then_inc(sem(f"hT_l{f}"), 1)

            chain = [0]

            def then(ins):
                chain[0] += 1
                ins.then_inc(sem("placing"), 1)
                dve.wait_ge(sem("placing"), chain[0])

            def place_picks():
                then(dve.tensor_scalar(tiles_f[:], base[:], float(P - 1), None, ALU.add))
                then(dve.tensor_copy(cnt_i[:], tiles_f[:]))
                then(dve.tensor_scalar(tiles_i[:], cnt_i[:], P.bit_length() - 1, None, ALU.arith_shift_right))
                then(dve.tensor_scalar(tiles_f[:], tiles_i[:], 1.0, None, ALU.max))
                then(dve.memset(bnd[:, 0:1], 0.0))
                then(dve.memset(bnd[:, 1:2], float(NT)))
                for e in range(E):
                    then(dve.tensor_tensor(bnd[:, e + 2:e + 3], bnd[:, e + 1:e + 2], tiles_f[:, e:e + 1], ALU.add))
                then(dve.tensor_scalar(cut[:, 0, :], bnd[:, 0:E + 1], 1.0, None, ALU.add))
                then(dve.tensor_scalar(cut[:, 1, :], bnd[:, 1:E + 2], -1.0, None, ALU.add))
                then(dve.tensor_tensor(cut[:, 0, :], cut[:, 0, :], cut[:, 1, :], ALU.min))
                then(dve.memset(cut[:, 0, E:E + 1], 0.0))
                then(dve.tensor_copy(table[:, 0:E + 2], bnd[:]))
                then(dve.tensor_copy(table[:, 16:16 + E], cut[:, 0, 1:E + 1]))
                then(dve.tensor_scalar(off[:], bnd[:, 1:E + 1], float(P), -float(P * NT), ALU.mult, ALU.add))
                for k in range(2):
                    for e in range(E):
                        then(dve.tensor_scalar(place[:, :, e], routes[:, :, k * E + e], off[:, e:e + 1], None, ALU.mult))
                    then(dve.tensor_reduce(where[:], place[:], AX, ALU.add))
                    then(dve.tensor_tensor(wherek[:], where[:], routes[:, :, 2 * E + k], ALU.add))
                    then(dve.tensor_copy(pos_i[:, k, :], wherek[:]))
                dve.tensor_copy(bnd[:, 0:1], bnd[:, 0:1]).then_inc(sem("table"), 1)

            pieces(0, (None, 0, 0), DC, SPLIT_GU)
            split_down(0)
            for g in range(UNPLACED):
                expert_tile(g)
            place_picks()
            with dve.Fori(UNPLACED, EARLY) as g:
                expert_tile(g)
            expert_tile(EARLY, (None, 1, 1))
            with dve.Fori(EARLY + 1, NT) as g:
                expert_tile(g)
            with dve.Fori(0, E // 2) as j:
                for k in range(2):
                    e = 2 * j + k
                    first = dve.value_load(table[0:1, bass.ds(e + 1, 1)], min_val=NT, max_val=MAX_TILES)
                    end = dve.value_load(table[0:1, bass.ds(e + 2, 1)], min_val=NT, max_val=MAX_TILES)
                    when = dve.value_load(table[0:1, bass.ds(e + 16, 1)], min_val=0, max_val=MAX_TILES)
                    split_down(e + 1)
                    with dve.Fori(first, end) as g:
                        expert_tile(g, (when, k, e + 2))


_INS = ['x', 'adj', 'L0_gnn_W_q', 'L0_gnn_b_q', 'L0_gnn_W_k', 'L0_gnn_b_k', 'L0_gnn_W_v', 'L0_gnn_b_v',
        'L0_ffn_Wr', 'L0_ffn_Wg_s', 'L0_ffn_Wu_s', 'L0_ffn_Wd_s', 'L0_ffn_Wg', 'L0_ffn_Wu', 'L0_ffn_Wd']
_OUTS = [((2048, 512), 'float32')]


def kernel(**inputs):
    import numpy as _np
    import concourse.bacc as _bacc
    from concourse import mybir as _mybir
    from concourse.bass_utils import run_bass_kernel_spmd as _run

    nc = _bacc.Bacc("TRN2", target_bir_lowering=False, num_devices=1)
    arrays, args = {}, []
    for name in _INS:
        a = _np.ascontiguousarray(inputs[name])
        arrays[f"in_{name}_dram"] = a
        args.append(nc.dram_tensor(f"in_{name}_dram", a.shape, _mybir.dt.from_np(a.dtype), kind="ExternalInput").ap())
    for i, (shape, dtype) in enumerate(_OUTS):
        dt = _mybir.dt.from_np(_np.dtype(dtype))
        args.append(nc.dram_tensor(f"out_{i}_dram", shape, dt, kind="ExternalOutput").ap())
    gnn_moe(nc, *args)
    r = _run(nc, [arrays], core_ids=[0])
    got = tuple(r.results[0][f"out_{i}_dram"] for i in range(len(_OUTS)))
    return got[0]
```

```python
from contextlib import ExitStack

import concourse.bass as bass
from concourse import mybir

F32 = mybir.dt.float32
F32R = mybir.dt.float32r
I32 = mybir.dt.int32
U32 = mybir.dt.uint32
ALU = mybir.AluOpType
ACT = mybir.ActivationFunctionType
AX = mybir.AxisListType.X

P = 128
LN_EPS = 1e-5
MASKED = -10000.0


def gnn_moe(nc, x, adj, w_q, b_q, w_k, b_k, w_v, b_v, w_r, wg_s, wu_s, wd_s, wg, wu, wd, out):
    T, D = x.shape
    E, _, F = wg.shape
    NT = T // P
    DC = D // P
    FC = F // P
    KB = T // 512
    KG = T // 512
    SCALE = 1.0 / float(D) ** 0.5
    STAGES = E + 1
    MAX_TILES = NT + 2 * T // P + E
    SLOT_TILES = MAX_TILES + 2
    PADS = -(-(SLOT_TILES - NT) // (NT - 2))
    ROW = D + 2
    assert PADS * (NT - 2) == SLOT_TILES - NT
    assert D == 512 and F == 1024 and E == 8 and NT == 16

    acc = nc.dram_tensor("acc", [T + P, D], F32, kind="Internal").ap()
    tokens = nc.dram_tensor("tokens", [T, ROW], F32, kind="Internal").ap()
    slots = nc.dram_tensor("slots", [(SLOT_TILES - NT) * P, ROW], F32, kind="Internal").ap()

    with ExitStack() as ctx:
        BASE = 16512

        def at(name, offset, shape, dtype=F32):
            return nc.alloc_sbuf_tensor_at(name, shape, dtype, offset=BASE + offset)

        K = 1024
        ctx.enter_context(nc.sbuf_tensor("arena", [P, 207 * K], mybir.dt.uint8))
        xnT = {"h": at("xnT_h", 0, [P, DC, T], F32R), "l": at("xnT_l", 32 * K, [P, DC, T], F32R)}
        v = {"h": at("v_h", 64 * K, [P, NT, D], F32R), "l": at("v_l", 96 * K, [P, NT, D], F32R)}
        A = {"h": at("A_h", 128 * K, [P, DC, D], F32R), "l": at("A_l", 136 * K, [P, DC, D], F32R)}
        yT = {"h": at("yT_h", 144 * K, [P, DC, 256], F32R), "l": at("yT_l", 148 * K, [P, DC, 256], F32R)}
        pT = {"h": at("pT_h", 152 * K, [P, 2, 512], F32R), "l": at("pT_l", 156 * K, [P, 2, 512], F32R)}
        adj_t = at("adj_t", 160 * K, [P, T])
        sc = at("sc", 168 * K, [P, 2, T])
        fill = at("fill", 184 * K, [P, 512])
        y_f = at("y_f", 186 * K, [P, 2, 256])
        x_t = at("x_t", 188 * K, [P, 2, D])
        x1 = at("x1", 192 * K, [P, D])
        x2T = at("x2T", 194 * K, [P, DC, P])
        x2row = at("x2row", 196 * K, [P, ROW])
        bv_row = at("bv_row", 198 * K + 64, [P, D])
        wk_raw = at("wk_raw", 168 * K, [P, DC, D])
        wq_raw = at("wq_raw", 176 * K, [P, DC, D])
        wv_raw = at("wv_raw", 160 * K, [P, DC, D])
        wq = {"h": at("wq_h", 64 * K, [P, DC, D], F32R), "l": at("wq_l", 72 * K, [P, DC, D], F32R)}
        wk = {"h": at("wk_h", 80 * K, [P, DC, D], F32R), "l": at("wk_l", 88 * K, [P, DC, D], F32R)}
        wvT = {"h": at("wvT_h", 144 * K, [P, DC, D], F32R), "l": at("wvT_l", 152 * K, [P, DC, D], F32R)}
        xn = at("xn", 184 * K, [P, 2, D])
        xT1 = {"h": at("xT1_h", 160 * K, [P, 2, DC, P], F32R), "l": at("xT1_l", 164 * K, [P, 2, DC, P], F32R)}
        padrow = at("padrow", 176 * K, [P, ROW])
        c2_rep = at("c2_rep", 194 * K, [P, D])
        spent = at("spent", 196 * K, [P, D])
        bk_rep = at("bk_rep", 192 * K, [P, DC, P])
        gu_h = [[at(f"gu{s}{m}_h", 64 * K * s + 32 * K * m, [P, DC, F], F32R) for m in range(2)] for s in range(2)]
        gu_l = [[at(f"gu{s}{m}_l", 64 * K * s + 32 * K * m + 16 * K, [P, DC, F], F32R) for m in range(2)] for s in range(2)]
        gu_raw = [[at(f"gu{s}{m}_raw", 64 * K * s + 32 * K * m + 16 * K, [P, DC, F]) for m in range(2)] for s in range(2)]
        gate_s_raw = at("gate_s_raw", 128 * K, [P, DC, F])
        dn_h = at("dn_h", 128 * K, [P, FC, D], F32R)
        dn_l = at("dn_l", 144 * K, [P, FC, D], F32R)
        dn_raw = at("dn_raw", 160 * K, [P, FC, D])
        e_x = at("e_x", 176 * K, [P, ROW])
        e_xT = {"h": at("e_xT_h", 179 * K, [P, DC, P], F32R), "l": at("e_xT_l", 181 * K, [P, DC, P], F32R)}
        hid = at("hid", 183 * K, [P, 2, 512])
        sil = at("sil", 187 * K, [P, 2, 512])
        hT = {"h": at("hT_h", 191 * K, [P, FC, P], F32R), "l": at("hT_l", 195 * K, [P, FC, P], F32R)}
        y = at("y", 199 * K, [P, D])
        send = at("send", 64 * K, [P, 4, ROW])
        small = [201 * K + 64]

        def keep(name, shape, dtype=F32):
            n = 4
            for k in shape[1:]:
                n *= k
            t = at(name, small[0], shape, dtype)
            small[0] += -(-n // 32) * 32
            assert small[0] <= 207 * K
            return t

        ident = keep("ident", [P, P])
        before = keep("before", [P, P])
        ones = keep("ones", [P, P])
        w_r_sb = keep("w_r_sb", [P, DC, E])
        bqk = keep("bqk", [P, 2, DC])
        c1 = keep("c1", [P, DC])
        bb = keep("bb", [P, 1])
        s_q = keep("s_q", [P, NT])
        iota8 = keep("iota8", [P, E])
        stat = keep("stat", [P, 6])
        mv = keep("mv", [P, 2, 2])
        var_e = keep("var_e", [P, 2])
        neg_half = keep("neg_half", [P, 1])
        rstd = keep("rstd", [P, 2])
        mx4 = keep("mx4", [P, KB])
        nmx = keep("nmx", [P, 2])
        den = keep("den", [P, 2])
        rden = keep("rden", [P, 1])
        lg = keep("lg", [P, E])
        tok = keep("tok", [P, NT], I32)
        nlm = keep("nlm", [P, 1])
        lex = keep("lex", [P, E])
        lsum = keep("lsum", [P, 1])
        lrs = keep("lrs", [P, 1])
        rw = keep("rw", [P, E])
        top = keep("top", [P, 8])
        topi = keep("topi", [P, 8], U32)
        topf = keep("topf", [P, 2])
        tdiff = keep("tdiff", [P, 1])
        tex = keep("tex", [P, 1])
        tsum = keep("tsum", [P, 1])
        route = keep("route", [P, 2 * E + 4])
        routes = keep("routes", [P, NT, 2 * E + 4])
        both = keep("both", [P, E])
        counts = keep("counts", [P, 2 * E])
        rank = keep("rank", [P, E])
        base = keep("base", [P, E])
        rsel = keep("rsel", [P, E])
        place = keep("place", [P, NT, E])
        where = keep("where", [P, NT])
        wherek = keep("wherek", [P, NT])
        pos_i = keep("pos_i", [P, 2, NT], I32)
        idx = keep("idx", [P, 4], I32)
        cnt_i = keep("cnt_i", [P, E], I32)
        tiles_i = keep("tiles_i", [P, E], I32)
        tiles_f = keep("tiles_f", [P, E])
        bnd = keep("bnd", [P, E + 2])
        off = keep("off", [P, E])
        cut = keep("cut", [P, 2, E + 1])
        table = keep("table", [P, 32], I32)
        meta_next = keep("meta_next", [P, 2])
        meta = keep("meta", [P, 2])

        bank = [ctx.enter_context(nc.psum_tensor(f"bank{n}", [P, 512], F32)) for n in range(8)]
        sems = {}

        def sem(name):
            if name not in sems:
                sems[name] = ctx.enter_context(nc.semaphore(name))
            return sems[name]

        def wait(eng, name, value):
            if isinstance(value, int) and value <= 0:
                return
            eng.wait_ge(sem(name), value)

        def wait_apart(eng, name, value):
            wait(eng, name, value)
            if not isinstance(value, int):
                eng.sem_inc(sem(f"waits_{eng.engine.name}"), 1)

        def rows(a, t):
            return a[bass.ds(t * P, P), :]

        PASSES = (("h", "h"), ("h", "l"), ("l", "h"))

        def product(pe, o, lhs, rhs, chunks, first=True, last=True):
            n = 0
            for c in chunks:
                for a, b in PASSES:
                    n += 1
                    mm = pe.matmul(o, lhs(a, c), rhs(b, c), start=first and n == 1,
                                   stop=last and n == 3 * len(chunks))
            return mm

        block = ctx.enter_context(nc.Block())

        SPLIT_GU = 2 * DC
        SPLIT_DN = 4
        UNPLACED = 2
        EARLY = 12

        def queries_follow(j, b, nxt):
            return nxt and b == 0 and (not isinstance(j, int) or j + 1 < NT // 2)

        @block.sync
        def _(sp):
            def load_x(t, b):
                sp.dma_start(x_t[:, b, :], rows(x, t)).then_inc(sem(f"x_in{b}"), 16)

            load_x(0, 0)
            load_x(1, 1)
            sp.dma_start(bqk[:, 0, :], b_q.rearrange("(p c) -> p c", c=DC)).then_inc(sem("in_b"), 16)
            sp.dma_start(bqk[:, 1, :], b_k.rearrange("(p c) -> p c", c=DC)).then_inc(sem("in_b"), 16)
            sp.dma_start(wq_raw[:], w_q.rearrange("(p c) n -> p c n", c=DC)).then_inc(sem("in_wq"), 16)
            sp.dma_start(wk_raw[:], w_k.rearrange("(p c) n -> p c n", c=DC)).then_inc(sem("in_wk"), 16)
            sp.dma_start(wv_raw[:], w_v.rearrange("(c p) n -> p c n", p=P)).then_inc(sem("in_wv"), 16)
            sp.dma_start(bv_row[:], b_v.rearrange("(a n) -> a n", a=1).broadcast_to([P, D])).then_inc(sem("in_bv"), 16)
            sp.dma_start(w_r_sb[:], w_r.rearrange("(c p) e -> p c e", p=P)).then_inc(sem("in_wr"), 16)

            sp.wait_ge(sem("pad"), 2)
            sp.dma_start(acc[T:T + P, :], padrow[:, 0:D]).then_inc(sem("pad_out"), 16)
            with sp.Fori(1, NT // 2) as j:
                for b in range(2):
                    wait(sp, "ln1_done", 2 * j + b - 1)
                    load_x(2 * j + b, b)
                    for k in range(PADS):
                        sp.dma_start(rows(slots, PADS * (2 * j + b - 2) + k), padrow[:]).then_inc(sem("pad_out"), 16)
            wait(sp, "ln1_done", NT)
            wait(sp, "v_ps", NT)
            wait(sp, "xnT_h", NT)
            wait(sp, "xnT_l", NT)
            sp.dma_start(adj_t[:], rows(adj, 0)).then_inc(sem("adj_in"), 16)

            def attention_step(i, b, after):
                if not isinstance(i, int) or i < NT - 1:
                    wait(sp, "scored", 4 * i + 4)
                    sp.dma_start(adj_t[:], rows(adj, i + 1)).then_inc(sem("adj_in"), 16)
                if not isinstance(i, int) or i < NT:
                    wait(sp, "x1_done", i - 1)
                    sp.dma_start(x_t[:, b, :], rows(x, i)).then_inc(sem(f"xr_in{b}"), 16)
                if after:
                    wait(sp, "x1_done", i)
                    sp.dma_start(rows(acc, i - 1), x1[:]).then_inc(sem("x1_out"), 16)
                    wait(sp, "x2_done", i)
                    wait(sp, "x2meta", i)
                    sp.dma_start(rows(tokens, i - 1), x2row[:]).then_inc(sem("x2_out"), 16)

            attention_step(0, 0, False)
            attention_step(1, 1, True)
            with sp.Fori(1, NT // 2 - 1) as j:
                attention_step(2 * j, 0, True)
                attention_step(2 * j + 1, 1, True)
            attention_step(NT - 2, 0, True)
            wait(sp, "y_ps", NT)
            sp.dma_start(gate_s_raw[:], wg_s.rearrange("(c p) f -> p c f", p=P)).then_inc(sem("gate_s_in"), 16)
            attention_step(NT - 1, 1, True)
            wait(sp, "scores", 4 * NT)
            sp.dma_start(gu_raw[0][1][:], wu_s.rearrange("(c p) f -> p c f", p=P)).then_inc(sem("gu_in0"), 16)
            wait(sp, "scored", 4 * NT)
            wait(sp, "p_turned", 4 * (NT - 1))
            sp.dma_start(dn_raw[:], wd_s.rearrange("(c p) d -> p c d", p=P)).then_inc(sem("dn_in"), 16)
            wait(sp, "p_turned", 4 * NT)
            sp.dma_start(e_x[:], rows(tokens, 0)).then_inc(sem("e_x_in"), 16)
            attention_step(NT, 0, True)
            wait(sp, "x2_out", 16 * NT)
            def load_send(t, k):
                sp.dma_start(send[:, k, :], rows(tokens, t)).then_inc(sem(f"send_in{k}"), 16)
            for k in range(4):
                load_send(k // 2, k)
            with sp.Fori(1, NT // 2) as j:
                for k in range(4):
                    sp.wait_ge(sem(f"sent{k}"), j * 16)
                    load_send(2 * j + k // 2, k)
            for k in range(4):
                sp.wait_ge(sem(f"sent{k}"), NT // 2 * 16)
            wait(sp, "table", 1)

            def load_gate_up(e, s):
                for m, w in enumerate((wg, wu)):
                    sp.dma_start(gu_raw[s][m][:], w[bass.ds(e, 1), :, :].rearrange("e (c p) f -> p (e c) f", p=P)).then_inc(sem(f"gu_in{s}"), 16)

            def load_down(e):
                wait(sp, "dn_l", SPLIT_DN * (e + 1))
                sp.dma_start(dn_raw[:], wd[bass.ds(e, 1), :, :].rearrange("e (c p) d -> p (e c) d", p=P)).then_inc(sem("dn_in"), 16)

            load_gate_up(0, 1)
            load_down(0)
            wait(sp, "up_done", NT)
            load_gate_up(1, 0)
            load_down(1)
            with sp.Fori(1, E // 2) as j:
                for s in range(2):
                    e = 2 * j + s
                    end = sp.value_load(table[0:1, bass.ds(e, 1)], min_val=NT, max_val=MAX_TILES)
                    wait(sp, "up_done", end)
                    load_gate_up(e, 1 - s)
                    load_down(e)
            n_tiles = sp.value_load(table[0:1, E + 1:E + 2], min_val=NT, max_val=MAX_TILES)
            wait(sp, "e_x_in", n_tiles * 16 + 32)
            wait(sp, "added", n_tiles * 16)
            half = T // 2
            sp.dma_start(out[0:half, :], acc[0:half, :]).then_inc(sem("out"), 16)
            sp.dma_start(out[half:T, :], acc[half:T, :]).then_inc(sem("out"), 16)
            sp.wait_ge(sem("out"), 32)

        @block.gpsimd
        def _(pool):
            pool.memset(ident[:], 0.0).then_inc(sem("pz"), 1)
            pool.memset(before[:], 1.0).then_inc(sem("pz"), 1)
            pool.memset(ones[:], 1.0).then_inc(sem("consts"), 1)
            pool.memset(neg_half[:], -0.5).then_inc(sem("consts"), 1)
            pool.memset(base[:], 0.0).then_inc(sem("consts"), 1)
            pool.iota(iota8[:], pattern=[[1, E]], base=0, channel_multiplier=0,
                      allow_small_or_imprecise_dtypes=True).then_inc(sem("consts"), 1)
            pool.iota(tok[:], pattern=[[P, NT]], base=0, channel_multiplier=1).then_inc(sem("tok"), 1)
            pool.wait_ge(sem("pz"), 2)
            pool.affine_select(out=ident[:], in_=ident[:], compare_op=ALU.not_equal, fill=1.0, base=0,
                               pattern=[[-1, P]], channel_multiplier=1).then_inc(sem("consts"), 1)
            pool.affine_select(out=before[:], in_=before[:], compare_op=ALU.is_gt, fill=0.0, base=0,
                               pattern=[[1, P]], channel_multiplier=-1).then_inc(sem("consts"), 1)

            def power(n, b):
                wait(pool, "var", n)
                pool.tensor_tensor(rstd[:, b:b + 1], var_e[:, b:b + 1], neg_half[:], ALU.pow).then_inc(sem("rstd"), 1)

            pool.wait_ge(sem("consts"), 6)
            power(1, 0)
            power(2, 1)
            pool.wait_ge(sem("c2_ps"), 1)
            pool.wait_ge(sem("wqk_l"), 2)
            pool.memset(padrow[:, 0:D + 1], 0.0).then_inc(sem("pad"), 1)
            pool.iota(padrow[:, D + 1:ROW].bitcast(I32), pattern=[[0, 1]], base=T, channel_multiplier=1).then_inc(sem("pad"), 1)
            with pool.Fori(0, NT // 2 - 1) as j:
                for b in range(2):
                    t = 2 * j + b
                    pool.wait_ge(sem("xT1_l"), t + 1)
                    pool.tensor_copy(xnT["l"][:, :, bass.ds(t * P, P)],
                                     xT1["l"][:, b, :, :].bitcast(F32)).then_inc(sem("xnT_l"), 1)
                    power(t + 3, b)
            for t in range(NT - 2, NT):
                for b in [t % 2]:
                    pool.wait_ge(sem("xT1_l"), t + 1)
                    pool.tensor_copy(xnT["l"][:, :, bass.ds(t * P, P)],
                                     xT1["l"][:, b, :, :].bitcast(F32)).then_inc(sem("xnT_l"), 1)
            pool.wait_ge(sem("tok"), 1)
            pool.memset(x2row[:, D:D + 1], 1.0).then_inc(sem("x2_weight"), 1)

            def label(t, b):
                wait(pool, "x2_out", t * 16)
                pool.tensor_copy(x2row[:, D + 1:ROW].bitcast(I32), tok[:, bass.ds(t, 1)]).then_inc(sem("x2meta"), 1)
                power(NT + t + 1, b)

            label(0, 0)
            label(1, 1)
            with pool.Fori(1, NT // 2) as j:
                label(2 * j, 0)
                label(2 * j + 1, 1)

            def add(g):
                wait_apart(pool, "y_done", g + 1)
                pool.indirect_dma_start(acc, bass.IndirectOffsetOnAxis(ap=meta[:, 1:2].bitcast(I32), axis=0),
                                        y[:], None, compute_op=ALU.add).then_inc(sem("added"), 16)
                pool.wait_ge(sem("added"), g * 16 + 16)

            pool.wait_ge(sem("pad_out"), 16 * (SLOT_TILES - NT + 1))
            with pool.Fori(0, UNPLACED) as g:
                add(g)
            pool.wait_ge(sem("table"), 1)
            with pool.Fori(0, NT // 2) as j:
                add(j + UNPLACED)
                for k in range(4):
                    n = 4 * j + k
                    t = 2 * j + k // 2
                    pool.wait_ge(sem(f"send_in{k}"), j * 16 + 16)
                    pool.tensor_copy(send[:, k, D:D + 1], routes[:, bass.ds(t, 1), 2 * E + 2 + k % 2]).then_inc(sem("addressed"), 1)
                    pool.tensor_copy(idx[:, k:k + 1], pos_i[:, k % 2, bass.ds(t, 1)]).then_inc(sem("addressed"), 1)
                    wait_apart(pool, "addressed", 2 * n + 2)
                    pool.indirect_dma_start(slots, bass.IndirectOffsetOnAxis(ap=idx[:, k:k + 1], axis=0),
                                            send[:, k, :], None).then_inc(sem(f"sent{k}"), 16)
            n_tiles = pool.value_load(table[0:1, E + 1:E + 2], min_val=NT, max_val=MAX_TILES)
            with pool.Fori(NT // 2 + UNPLACED, n_tiles) as g:
                add(g)

        @block.tensor
        def _(pe):
            pe.wait_ge(sem("consts"), 6)
            pe.wait_ge(sem("bk_rep"), DC)
            pe.wait_ge(sem("in_wq"), 16)
            for o in range(DC):
                mm = pe.matmul(bank[6][:], bk_rep[:, o, :], wq_raw[:, o, :], start=o == 0, stop=o == DC - 1)
            mm.then_inc(sem("c2_ps"), 1)
            pe.wait_ge(sem("in_wv"), 16)
            for c in range(DC):
                for o in range(DC):
                    mm = pe.transpose(bank[c][:, o * P:(o + 1) * P], wv_raw[:, o, c * P:(c + 1) * P], ident[:])
                mm.then_inc(sem("wv_turned"), 1)
            pe.wait_ge(sem("wqk_l"), 2)

            def A_chunk(c):
                product(pe, bank[4 + c][:], lambda a, o: wq[a][:, o, c * P:(c + 1) * P],
                        lambda b, o: wk[b][:, o, :], range(DC)).then_inc(sem("A_ps"), 1)

            def before_attention(t, b, this, prev):
                if this:
                    wait(pe, "ln1_done", t + 1)
                    wait(pe, "xT1_l", t - 1)
                    for c in range(DC):
                        mm = pe.transpose(bank[b][:, c * P:(c + 1) * P], xn[:, b, c * P:(c + 1) * P], ident[:])
                    mm.then_inc(sem("xn_turned"), 1)
                if prev:
                    wait(pe, "xT1_l", t)
                    wait(pe, "v_l", t - 2)
                    product(pe, bank[3 - b][:], lambda a, c: xT1[a][:, 1 - b, c, :],
                            lambda b_, c: wvT[b_][:, c, :], range(DC)).then_inc(sem("v_ps"), 1)

            A_chunk(0)
            A_chunk(1)
            pe.wait_ge(sem("wvT_l"), DC)
            before_attention(0, 0, True, False)
            pe.wait_ge(sem("c2_done"), 1)
            A_chunk(2)
            A_chunk(3)
            before_attention(1, 1, True, True)
            pe.wait_ge(sem("in_b"), 32)
            pe.wait_ge(sem("A_done"), 1)
            for c in range(DC + 1):
                for o in range(DC):
                    lhs = wk_raw[:, o, c * P:(c + 1) * P] if c < DC else bk_rep[:, o, :]
                    mm = pe.matmul(bank[4][:, 2 * c:2 * c + 2], lhs, bqk[:, :, o], start=o == 0, stop=o == DC - 1)
                if c == 1:
                    before_attention(2, 0, True, True)
            mm.then_inc(sem("biases"), 1)
            before_attention(3, 1, True, True)
            with pe.Fori(2, NT // 2) as j:
                before_attention(2 * j, 0, True, True)
                before_attention(2 * j + 1, 1, True, True)
            before_attention(NT, 0, False, True)

            def queries(j, half):
                for c in range(2):
                    m = 2 * half + c
                    mm = product(pe, bank[7][:, c * 256:(c + 1) * 256], lambda a, d: A[a][:, d, m * P:(m + 1) * P],
                                 lambda b, d: xnT[b][:, d, bass.ds(j * 256, 256)], range(DC))
                mm.then_inc(sem("y_ps"), 1)

            def scores(i, b, n):
                wait(pe, "scored", 4 * (i - 1) + n + 1)
                product(pe, bank[n][:], lambda a, c: yT[a][:, c, b * P:(b + 1) * P],
                        lambda b_, c: xnT[b_][:, c, n * 512:(n + 1) * 512], range(DC)).then_inc(sem("scores"), 1)

            def turn(i, b, g):
                wait(pe, "exp_done", i + 1)
                wait(pe, "pT_l", 4 * i + g - 1)
                for c in range(4):
                    k = 4 * g + c
                    mm = pe.transpose(bank[4 + g % 2][:, c * P:(c + 1) * P], sc[:, b, k * P:(k + 1) * P], ident[:])
                mm.then_inc(sem("p_turned"), 1)

            def attend(i, g):
                wait(pe, "pT_l", 4 * i + g + 1)
                if g == 0:
                    wait(pe, "o_done", i)
                product(pe, bank[6][:], lambda a, c: pT[a][:, g % 2, c * P:(c + 1) * P],
                        lambda b, c: v[b][:, 4 * g + c, :], range(4), first=g == 0, last=g == 3
                        ).then_inc(sem("attended"), 1)

            def turn_normalised(i):
                wait(pe, "x2_done", i)
                wait(pe, "counts_read", i - 1)
                for c in range(DC):
                    mm = pe.transpose(bank[7][:, c * P:(c + 1) * P], x2row[:, c * P:(c + 1) * P], ident[:])
                mm.then_inc(sem("x2_turned"), 1)

            def route_logits(i):
                wait(pe, "x2T_done", i)
                for c in range(DC):
                    mm = pe.matmul(bank[7][:, 0:E], x2T[:, c, :], w_r_sb[:, c, :], start=c == 0, stop=c == DC - 1)
                mm.then_inc(sem("logits"), 1)

            def count_picks(i):
                wait(pe, "logits_read", i)
                wait(pe, "picked", i)
                pe.matmul(bank[7][:, 0:E], before[:], both[:], start=True, stop=True)
                pe.matmul(bank[7][:, E:2 * E], ones[:], both[:], start=True, stop=True).then_inc(sem("counted"), 1)

            def attention_step(j, b, this=True, nxt=True, prev=True):
                i = 2 * j + b
                if nxt:
                    if b == 1:
                        wait(pe, "yT_l", 2 * j + 4)
                    scores(i + 1, 1 - b, 0)
                    scores(i + 1, 1 - b, 1)
                if this:
                    turn(i, b, 0)
                    turn(i, b, 1)
                if prev:
                    turn_normalised(i)
                if nxt:
                    scores(i + 1, 1 - b, 2)
                if prev:
                    route_logits(i)
                if nxt:
                    scores(i + 1, 1 - b, 3)
                ahead = queries_follow(j, b, nxt)
                if ahead:
                    if prev:
                        wait(pe, "logits_read", i)
                    queries(j + 1, 0)
                if this:
                    attend(i, 0)
                    turn(i, b, 2)
                    attend(i, 1)
                if ahead:
                    wait(pe, "yT_f", 2 * j + 3)
                    queries(j + 1, 1)
                if this:
                    turn(i, b, 3)
                    attend(i, 2)
                    attend(i, 3)
                if prev:
                    if ahead:
                        wait(pe, "yT_f", 2 * j + 4)
                    count_picks(i)

            def turn_rows(g):
                wait(pe, "e_x_in", g * 16 + 16)
                wait(pe, "e_xT_l", g)
                for c in range(DC):
                    mm = pe.transpose(bank[7][:, c * P:(c + 1) * P], e_x[:, c * P:(c + 1) * P], ident[:])
                mm.then_inc(sem("x_turned"), 1)

            pe.wait_ge(sem("xnT_h"), NT)
            pe.wait_ge(sem("xnT_l"), NT)
            pe.wait_ge(sem("v_l"), NT)
            pe.wait_ge(sem("c1_done"), 2)
            pe.wait_ge(sem("A_done"), DC)
            queries(0, 0)
            pe.wait_ge(sem("yT_f"), 1)
            queries(0, 1)
            pe.wait_ge(sem("yT_l"), 2)
            for n in range(KB):
                scores(0, 0, n)
            attention_step(0, 0, prev=False)
            attention_step(0, 1)
            with pe.Fori(1, NT // 2 - 1) as j:
                attention_step(j, 0)
                attention_step(j, 1)
            attention_step(NT // 2 - 1, 0)
            attention_step(NT // 2 - 1, 1, nxt=False)
            wait(pe, "counts_read", NT - 1)
            turn_rows(0)

            def expert_tile(g, s, downs, route=False):
                def project(m, f, read):
                    wait(pe, read, g)
                    n = 2 * f + m
                    return product(pe, bank[n][:], lambda a, c: e_xT[a][:, c, :],
                                   lambda b, c: (gu_h if b == "h" else gu_l)[s][m][:, c, f * 512:(f + 1) * 512], range(DC))

                def turn_hidden(f):
                    wait(pe, f"hid{f}", g + 1)
                    wait(pe, f"hT_l{f}", g)
                    for c in range(4):
                        mm = pe.transpose(bank[4 + f][:, c * P:(c + 1) * P], hid[:, f, c * P:(c + 1) * P], ident[:])
                    mm.then_inc(sem(f"h_turned{f}"), 1)

                def down(chunks):
                    return product(pe, bank[6][:], lambda a, c: hT[a][:, c, :],
                                   lambda b, c: (dn_h if b == "h" else dn_l)[:, c, :], chunks,
                                   first=chunks[0] == 0, last=chunks[-1] == FC - 1)

                wait(pe, "e_xT_l", g + 1)
                project(0, 0, "silu0").then_inc(sem("gate0"), 1)
                project(1, 0, "hid0").then_inc(sem("up0"), 1)
                if route:
                    turn_normalised(NT)
                project(0, 1, "silu1").then_inc(sem("gate1"), 1)
                if route:
                    route_logits(NT)
                turn_hidden(0)
                project(1, 1, "hid1").then_inc(sem("up_done"), 1)
                wait(pe, "hT_l0", g + 1)
                wait(pe, "y_done", g)
                wait(pe, "dn_l", downs)
                down(range(0, 2))
                turn_hidden(1)
                if route:
                    count_picks(NT)
                down(range(2, 4))
                if route:
                    wait(pe, "counts_read", NT)
                turn_rows(g + 1)
                wait(pe, "hT_l1", g + 1)
                down(range(4, FC)).then_inc(sem("down_done"), 1)

            pe.wait_ge(sem("gu_l"), SPLIT_GU)
            expert_tile(0, 0, SPLIT_DN, True)
            with pe.Fori(1, NT) as g:
                expert_tile(g, 0, SPLIT_DN)
            pe.wait_ge(sem("table"), 1)
            with pe.Fori(0, E // 2) as j:
                for k in range(2):
                    e = 2 * j + k
                    first = pe.value_load(table[0:1, bass.ds(e + 1, 1)], min_val=NT, max_val=MAX_TILES)
                    end = pe.value_load(table[0:1, bass.ds(e + 2, 1)], min_val=NT, max_val=MAX_TILES)
                    wait_apart(pe, "gu_l", e * SPLIT_GU + 2 * SPLIT_GU)
                    with pe.Fori(first, end) as g:
                        expert_tile(g, 1 - k, e * SPLIT_DN + 2 * SPLIT_DN)

        @block.scalar
        def _(act):
            def copy(o, i, scale=None):
                return act.activation(o, i, ACT.Copy) if scale is None else act.activation(o, i, ACT.Copy, scale=scale)

            act.wait_ge(sem("in_wq"), 16)
            copy(wq["h"][:], wq_raw[:]).then_inc(sem("wqk_h"), 1)
            act.wait_ge(sem("in_wk"), 16)
            copy(wk["h"][:], wk_raw[:]).then_inc(sem("wqk_h"), 1)
            for c in range(DC):
                wait(act, "wv_turned", c + 1)
                copy(wvT["h"][:, c, :], bank[c][:]).then_inc(sem("wvT_h"), 1)

            def A_chunks(m, n):
                for c in range(m, n):
                    wait(act, "A_ps", c + 1)
                    copy(A["h"][:, c, :], bank[4 + c][:]).then_inc(sem("A_h"), 1)

            A_chunks(0, 2)
            act.wait_ge(sem("wv_turned"), DC)

            def before_attention(t, b, this, prev):
                if this:
                    wait(act, "xn_turned", t + 1)
                    wait(act, "v_ps", t - 1)
                    wait(act, "xnT_h", t - 1)
                    wait(act, "xT1_l", t - 1)
                    copy(xT1["h"][:, b, :, :], bank[b][:].rearrange("p (c q) -> p c q", c=DC)).then_inc(sem("xT1_h"), 1)
                    wait(act, "xT1_h", t + 1)
                    copy(xnT["h"][:, :, bass.ds(t * P, P)], xT1["h"][:, b, :, :].bitcast(F32)).then_inc(sem("xnT_h"), 1)
                if prev:
                    wait(act, "v_ps", t)
                    copy(v["h"][:, bass.ds(t - 1, 1), :], bank[3 - b][:].rearrange("p (a n) -> p a n", a=1)).then_inc(sem("v_h"), 1)

            before_attention(0, 0, True, False)
            A_chunks(2, DC)
            before_attention(1, 1, True, True)
            before_attention(2, 0, True, True)
            before_attention(3, 1, True, True)
            with act.Fori(2, NT // 2) as j:
                before_attention(2 * j, 0, True, True)
                before_attention(2 * j + 1, 1, True, True)
            before_attention(NT, 0, False, True)

            def pieces(g, split, n, m):
                if split is None:
                    return
                when, s, filling = split
                if when is not None:
                    with act.If(g == when):
                        pieces(g, (None, s, filling), n, m)
                    return
                shared = isinstance(filling, int) and filling == 0
                if n == 0 and shared:
                    wait(act, "gate_s_in", 16)
                    wait(act, "scores", 4 * NT)
                else:
                    wait(act, f"gu_in{s}", filling * 32 + (16 if s == 0 else 0))
                for k in range(n, m):
                    raw = gate_s_raw if shared and k < DC else gu_raw[s][k // DC]
                    copy(gu_h[s][k // DC][:, k % DC, :], raw[:, k % DC, :]).then_inc(sem("gu_h"), 1)

            def turned_rows(g):
                wait(act, "x_turned", g + 1)
                wait(act, "up_done", g)
                wait(act, "e_xT_l", g)
                copy(e_xT["h"][:], bank[7][:].rearrange("p (c q) -> p c q", c=DC)).then_inc(sem("e_xT_h"), 1)

            def queries(n, half):
                wait(act, "yT_f", n + 1)
                copy(yT["h"][:, 2 * half:2 * half + 2, :], y_f[:]).then_inc(sem("yT_h"), 1)

            def probabilities(i, b):
                wait(act, "nmx_done", i + 1)
                act.activation(sc[:, b, :], sc[:, b, :], ACT.Exp, bias=nmx[:, b:b + 1],
                               accum_out=den[:, b:b + 1]).then_inc(sem("exp_done"), 1)

            def group(i, g):
                n = 4 * i + g
                wait(act, "p_turned", n + 1)
                wait(act, "attended", n - 1)
                wait(act, "pT_l", n - 1)
                copy(pT["h"][:, g % 2, :], bank[4 + g % 2][:]).then_inc(sem("pT_h"), 1)

            def keep_turned(i):
                wait(act, "x2_turned", i)
                wait(act, "logits", i - 1)
                copy(x2T[:], bank[7][:].rearrange("p (c q) -> p c q", c=DC)).then_inc(sem("x2T_done"), 1)

            def router_exp(i):
                wait(act, "nlm_done", i)
                act.activation(lex[:], lg[:], ACT.Exp, bias=nlm[:], accum_out=lsum[:]).then_inc(sem("lex_done"), 1)

            def pick_exp(i):
                wait(act, "tdiff_done", i)
                act.activation(tex[:], tdiff[:], ACT.Exp).then_inc(sem("tex_done"), 1)

            def attention_step(j, b, this=True, nxt=True, prev=True):
                i = 2 * j + b
                if this:
                    group(i, 0)
                    group(i, 1)
                if prev:
                    keep_turned(i)
                    router_exp(i)
                if not nxt:
                    pieces(0, (None, 0, 0), 0, 3)
                ahead = queries_follow(j, b, nxt)
                if ahead:
                    queries(2 * j + 2, 0)
                if prev:
                    pick_exp(i)
                if this:
                    group(i, 2)
                if not nxt:
                    pieces(0, (None, 0, 0), 3, 5)
                if ahead:
                    queries(2 * j + 3, 1)
                if this:
                    group(i, 3)
                if not nxt:
                    pieces(0, (None, 0, 0), 5, SPLIT_GU)
                if nxt:
                    probabilities(i + 1, 1 - b)

            queries(0, 0)
            queries(1, 1)
            probabilities(0, 0)
            attention_step(0, 0, prev=False)
            attention_step(0, 1)
            with act.Fori(1, NT // 2 - 1) as j:
                attention_step(j, 0)
                attention_step(j, 1)
            attention_step(NT // 2 - 1, 0)
            attention_step(NT // 2 - 1, 1, nxt=False)
            turned_rows(0)
            wait(act, "meta_next", 1)
            act.dma_start(e_x[:], rows(tokens, 1)).then_inc(sem("e_x_in"), 16)

            def split_down(stage, first, m=0, n=SPLIT_DN):
                wait(act, "dn_in", stage * 16 + 16)
                wait(act, "down_done", first)
                for c in range(m, n):
                    k = FC // SPLIT_DN
                    copy(dn_h[:, c * k:(c + 1) * k, :], dn_raw[:, c * k:(c + 1) * k, :]).then_inc(sem("dn_h"), 1)

            def expert_tile(g, source, row, split=None, route=False):
                for f in range(2):
                    wait(act, f"gate{f}", g + 1)
                    wait(act, f"hid{f}", g)
                    if route:
                        wait(act, "x1_done", NT)
                    act.activation(sil[:, f, :], bank[2 * f][:], ACT.Silu).then_inc(sem(f"silu{f}"), 1)
                    if f == 0:
                        pieces(g, split, 0, 3)
                        if route:
                            keep_turned(NT)
                if route:
                    wait(act, "x1_out", 16 * NT)
                    wait(act, "x2_out", 16 * NT)
                    wait(act, "x2_turned", NT)
                    wait(act, "logits", NT)
                for f in range(2):
                    wait(act, f"h_turned{f}", g + 1)
                    wait(act, "down_done", g)
                    wait(act, f"hT_l{f}", g)
                    copy(hT["h"][:, 4 * f:4 * f + 4, :], bank[4 + f][:].rearrange("p (c q) -> p c q", c=4)
                         ).then_inc(sem(f"hT_h{f}"), 1)
                    if f == 0:
                        pieces(g, split, 3, 6)
                        if route:
                            router_exp(NT)
                            pick_exp(NT)
                turned_rows(g + 1)
                wait(act, "meta_next", g + 2)
                act.dma_start(e_x[:], rows(source, row)).then_inc(sem("e_x_in"), 16)
                wait(act, "down_done", g + 1)
                wait(act, "meta", g + 1)
                wait(act, "added", g * 16)
                copy(y[:], bank[6][:], scale=meta[:, 0:1]).then_inc(sem("y_done"), 1)
                pieces(g, split, 6, SPLIT_GU)

            split_down(0, 0)
            expert_tile(0, tokens, 2, None, True)
            with act.Fori(1, EARLY) as g:
                expert_tile(g, tokens, g + 2)
            expert_tile(EARLY, tokens, EARLY + 2, (None, 1, 1))
            with act.Fori(EARLY + 1, NT - 2) as g:
                expert_tile(g, tokens, g + 2)
            for k in range(4):
                act.wait_ge(sem(f"sent{k}"), NT // 2 * 16)
            expert_tile(NT - 2, slots, 0)
            expert_tile(NT - 1, slots, 1)
            act.wait_ge(sem("table"), 1)
            with act.Fori(0, E // 2) as j:
                for k in range(2):
                    e = 2 * j + k
                    first = act.value_load(table[0:1, bass.ds(e + 1, 1)], min_val=NT, max_val=MAX_TILES)
                    end = act.value_load(table[0:1, bass.ds(e + 2, 1)], min_val=NT, max_val=MAX_TILES)
                    when = act.value_load(table[0:1, bass.ds(e + 16, 1)], min_val=0, max_val=MAX_TILES)
                    split_down(e + 1, first)
                    with act.Fori(first, end) as g:
                        expert_tile(g, slots, g + 2 - NT, (when, k, j + 1 + k))

        @block.vector
        def _(dve):
            def minus(o, a, b):
                return dve.tensor_tensor(o, a, b.bitcast(F32), ALU.subtract)

            def statistics(a, n, b):
                dve.bn_stats(stat[:], a).then_inc(sem("stat"), 1)
                wait_apart(dve, "stat", n)
                dve.bn_aggr(mv[:, b, :], stat[:]).then_inc(sem("mean_var"), 1)
                wait(dve, "mean_var", n)
                dve.tensor_scalar(var_e[:, b:b + 1], mv[:, b, 1:2], LN_EPS, None, ALU.add).then_inc(sem("var"), 1)

            def normalise(o, a, n, b):
                wait(dve, "rstd", n)
                return dve.tensor_scalar(o, a, mv[:, b, 0:1], rstd[:, b:b + 1], ALU.subtract, ALU.mult)

            def measure(t, b, j):
                dve.wait_ge(sem(f"x_in{b}"), j * 16 + 16)
                wait(dve, "ln1_done", t - 1)
                statistics(x_t[:, b, :], t + 1, b)

            def layer_norm(t, b):
                wait(dve, "xn_turned", t - 1)
                normalise(xn[:, b, :], x_t[:, b, :], t + 1, b).then_inc(sem("ln1_done"), 1)

            measure(0, 0, 0)
            measure(1, 1, 0)
            layer_norm(0, 0)
            dve.wait_ge(sem("consts"), 6)
            dve.wait_ge(sem("in_b"), 32)
            for c in range(DC):
                dve.tensor_scalar(bk_rep[:, c, :], ones[:], bqk[:, 1, c:c + 1], None, ALU.mult).then_inc(sem("bk_rep"), 1)
            dve.wait_ge(sem("wqk_h"), 1)
            minus(wq["l"][:], wq_raw[:], wq["h"][:]).then_inc(sem("wqk_l"), 1)
            dve.wait_ge(sem("wqk_h"), 2)
            minus(wk["l"][:], wk_raw[:], wk["h"][:]).then_inc(sem("wqk_l"), 1)
            dve.wait_ge(sem("c2_ps"), 1)
            dve.tensor_copy(c2_rep[:], bank[6][:]).then_inc(sem("c2_done"), 1)
            for c in range(DC):
                dve.wait_ge(sem("wvT_h"), c + 1)
                minus(wvT["l"][:, c, :], bank[c][:], wvT["h"][:, c, :]).then_inc(sem("wvT_l"), 1)

            def A_chunks(m, n):
                for c in range(m, n):
                    dve.wait_ge(sem("A_h"), c + 1)
                    minus(A["l"][:, c, :], bank[4 + c][:], A["h"][:, c, :]).then_inc(sem("A_done"), 1)

            A_chunks(0, 2)
            dve.wait_ge(sem("c2_done"), 1)

            def keep_bias(t):
                wait(dve, "sq_sum", t + 1)
                dve.tensor_copy(s_q[:, bass.ds(t, 1)], tsum[:]).then_inc(sem("sq_done"), 1)

            def before_attention(t, b, this, prev, j, further=True):
                if this:
                    wait(dve, "xT1_h", t + 1)
                    wait(dve, "xnT_l", t - 1)
                    wait(dve, "v_ps", t - 1)
                    minus(xT1["l"][:, b, :, :], bank[b][:].rearrange("p (c q) -> p c q", c=DC),
                          xT1["h"][:, b, :, :]).then_inc(sem("xT1_l"), 1)
                if prev:
                    keep_bias(t - 1)
                if this and (further or b == 0):
                    layer_norm(t + 1, 1 - b)
                if this:
                    wait(dve, "sq_done", t)
                    wait_apart(dve, "ln1_done", t + 1)
                    dve.tensor_tensor_reduce(out=spent[:], in0=xn[:, b, :], in1=c2_rep[:], scale=1.0, scalar=0.0,
                                             op0=ALU.mult, op1=ALU.add, accum_out=tsum[:]).then_inc(sem("sq_sum"), 1)
                if prev:
                    wait(dve, "v_h", t)
                    minus(v["l"][:, bass.ds(t - 1, 1), :], bank[3 - b][:].rearrange("p (a n) -> p a n", a=1),
                          v["h"][:, bass.ds(t - 1, 1), :]).then_inc(sem("v_l"), 1)
                if further:
                    measure(t + 2, b, j + 1)

            before_attention(0, 0, True, False, 0)
            A_chunks(2, DC)
            before_attention(1, 1, True, True, 0)
            before_attention(2, 0, True, True, 1)
            before_attention(3, 1, True, True, 1)
            with dve.Fori(2, NT // 2 - 1) as j:
                before_attention(2 * j, 0, True, True, j)
                before_attention(2 * j + 1, 1, True, True, j)
            before_attention(NT - 2, 0, True, True, NT // 2 - 1, False)
            before_attention(NT - 1, 1, True, True, NT // 2 - 1, False)
            dve.wait_ge(sem("biases"), 1)
            dve.tensor_copy(c1[:], bank[4][:, 0:2 * DC].rearrange("p (c a) -> p c a", a=2)[:, :, 0]).then_inc(sem("c1_done"), 1)
            dve.tensor_copy(bb[:], bank[4][:, 2 * DC:2 * DC + 1]).then_inc(sem("c1_done"), 1)
            before_attention(NT, 0, False, True, NT // 2, False)
            dve.wait_ge(sem("sq_done"), NT)
            dve.wait_ge(sem("c1_done"), 2)
            dve.tensor_scalar(s_q[:], s_q[:], bb[:, 0:1], SCALE, ALU.add, ALU.mult).then_inc(sem("sq_done"), 1)
            dve.wait_ge(sem("sq_done"), NT + 1)

            def pieces(g, split, n, m):
                if split is None:
                    return
                when, s, stage = split
                if when is not None:
                    with dve.If(g == when):
                        pieces(g, (None, s, stage), n, m)
                    return
                for k in range(n, m):
                    wait(dve, "gu_h", stage * SPLIT_GU + k + 1)
                    raw = gate_s_raw if isinstance(stage, int) and stage == 0 and k < DC else gu_raw[s][k // DC]
                    minus(gu_l[s][k // DC][:, k % DC, :], raw[:, k % DC, :],
                          gu_h[s][k // DC][:, k % DC, :]).then_inc(sem("gu_l"), 1)

            def turned_rows(g):
                wait(dve, "e_x_in", g * 16 + 16)
                wait(dve, "meta", g)
                dve.tensor_copy(meta_next[:].bitcast(I32), e_x[:, D:ROW].bitcast(I32)).then_inc(sem("meta_next"), 1)
                wait(dve, "e_xT_h", g + 1)
                minus(e_xT["l"][:], bank[7][:].rearrange("p (c q) -> p c q", c=DC), e_xT["h"][:]).then_inc(sem("e_xT_l"), 1)

            def queries(n, half):
                wait(dve, "y_ps", n + 1)
                wait(dve, "yT_h", n)
                wait(dve, "yT_l", n)
                for c in range(2):
                    m = 2 * half + c
                    ins = dve.tensor_scalar(y_f[:, c, :], bank[7][:, c * 256:(c + 1) * 256], c1[:, m:m + 1], SCALE,
                                            ALU.add, ALU.mult)
                ins.then_inc(sem("yT_f"), 1)
                wait(dve, "yT_h", n + 1)
                minus(yT["l"][:, 2 * half:2 * half + 2, :], y_f[:], yT["h"][:, 2 * half:2 * half + 2, :]).then_inc(sem("yT_l"), 1)

            def mask(i, b, n):
                wait(dve, "scores", 4 * i + n + 1)
                if n == 0:
                    wait(dve, "adj_in", i * 16 + 16)
                    wait(dve, "p_turned", 4 * (i - 1))
                dve.scalar_tensor_tensor(out=sc[:, b, n * 512:(n + 1) * 512], in0=bank[n][:], scalar=s_q[:, bass.ds(i, 1)],
                                         in1=adj_t[:, n * 512:(n + 1) * 512], op0=ALU.add, op1=ALU.mult
                                         ).then_inc(sem("scored"), 1)

            def fill_zeros(i, b, n):
                part = sc[:, b, n * 512:(n + 1) * 512]
                wait(dve, "scored", 4 * i + n + 1)
                wait(dve, "filled", 4 * i + n)
                dve.tensor_scalar(fill[:], part, 0.0, MASKED, ALU.is_equal, ALU.mult).then_inc(sem("zeros"), 1)
                if n == 0:
                    wait(dve, "nmx_done", i)
                wait_apart(dve, "zeros", 4 * i + n + 1)
                dve.tensor_tensor_reduce(out=part, in0=part, in1=fill[:], scale=1.0, scalar=-3.0e38, op0=ALU.add,
                                         op1=ALU.max, accum_out=mx4[:, n:n + 1]).then_inc(sem("filled"), 1)

            def row_max(i, b):
                wait(dve, "filled", 4 * i + 4)
                wait(dve, "exp_done", i - 1)
                dve.tensor_reduce(nmx[:, b:b + 1], mx4[:], AX, ALU.max, negate=True).then_inc(sem("nmx_done"), 1)

            def group(i, g):
                n = 4 * i + g
                wait(dve, "pT_h", n + 1)
                minus(pT["l"][:, g % 2, :], bank[4 + g % 2][:], pT["h"][:, g % 2, :]).then_inc(sem("pT_l"), 1)

            def residual(i, b, n):
                wait(dve, "exp_done", i)
                wait(dve, "o_done", i - 1)
                dve.reciprocal(rden[:], den[:, 1 - b:2 - b]).then_inc(sem("rden_done"), 1)
                wait(dve, "attended", 4 * i)
                wait(dve, "x1_out", 16 * (i - 1))
                wait(dve, "x2_done", i - 1)
                wait(dve, "rden_done", i)
                dve.scalar_tensor_tensor(out=x1[:], in0=bank[6][:], scalar=rden[:, 0:1], in1=bv_row[:], op0=ALU.mult,
                                         op1=ALU.add).then_inc(sem("o_done"), 1)
                dve.wait_ge(sem(f"xr_in{1 - b}"), n * 16)
                wait(dve, "o_done", i)
                dve.scalar_tensor_tensor(out=x1[:], in0=x1[:], scalar=0.0, in1=x_t[:, 1 - b, :], op0=ALU.max,
                                         op1=ALU.add).then_inc(sem("x1_done"), 1)
                wait(dve, "x1_done", i)
                statistics(x1[:], NT + i, 1 - b)
                wait(dve, "x2_out", 16 * (i - 1))
                wait(dve, "x2_turned", i - 1)
                normalise(x2row[:, 0:D], x1[:], NT + i, 1 - b).then_inc(sem("x2_done"), 1)

            ROUTER = 15

            def logits(i):
                wait(dve, "logits", i)
                dve.tensor_copy(lg[:], bank[7][:, 0:E]).then_inc(sem("logits_read"), 1)
                wait(dve, "logits_read", i)
                dve.tensor_reduce(nlm[:], lg[:], AX, ALU.max, negate=True).then_inc(sem("nlm_done"), 1)

            steps = [0]

            def then_route(i, ins):
                steps[0] += 1
                ins.then_inc(sem("routing"), 1)
                wait_apart(dve, "routing", (i - 1) * ROUTER + steps[0])

            def picks(i):
                steps[0] = 0
                wait(dve, "lex_done", i)
                then_route(i, dve.reciprocal(lrs[:], lsum[:]))
                then_route(i, dve.tensor_scalar(rw[:], lex[:], lrs[:, 0:1], None, ALU.mult))
                then_route(i, dve.max(top[:], rw[:]))
                then_route(i, dve.max_index(topi[:], top[:], rw[:]))
                dve.tensor_tensor(tdiff[:], top[:, 1:2], top[:, 0:1], ALU.subtract).then_inc(sem("tdiff_done"), 1)
                then_route(i, dve.tensor_copy(topf[:], topi[:, 0:2]))
                for k in range(2):
                    then_route(i, dve.tensor_scalar(route[:, k * E:(k + 1) * E], iota8[:], topf[:, k:k + 1], None, ALU.is_equal))
                dve.tensor_tensor(both[:], route[:, 0:E], route[:, E:2 * E], ALU.add).then_inc(sem("picked"), 1)

            def pick_weights(i):
                wait(dve, "tex_done", i)
                then_route(i, dve.tensor_scalar(tsum[:], tex[:], 1.0, None, ALU.add))
                then_route(i, dve.reciprocal(route[:, 2 * E + 2:2 * E + 3], tsum[:]))
                then_route(i, dve.tensor_tensor(route[:, 2 * E + 3:2 * E + 4], tex[:], route[:, 2 * E + 2:2 * E + 3], ALU.mult))

            def take_counts(i):
                wait(dve, "counted", i)
                dve.tensor_copy(counts[:], bank[7][:, 0:2 * E]).then_inc(sem("counts_read"), 1)

            def ranks(i):
                steps[0] = ROUTER - 5
                wait(dve, "counts_read", i)
                then_route(i, dve.tensor_tensor(rank[:], counts[:, 0:E], base[:], ALU.add))
                for k in range(2):
                    then_route(i, dve.tensor_tensor_reduce(out=rsel[:], in0=route[:, k * E:(k + 1) * E], in1=rank[:], scale=1.0,
                                                           scalar=0.0, op0=ALU.mult, op1=ALU.add,
                                                           accum_out=route[:, 2 * E + k:2 * E + k + 1]))
                then_route(i, dve.tensor_copy(routes[:, bass.ds(i - 1, 1), :], route[:].rearrange("p (a n) -> p a n", a=1)))
                then_route(i, dve.tensor_tensor(base[:], base[:], counts[:, E:2 * E], ALU.add))
                assert steps[0] == ROUTER

            def attention_step(j, b, this=True, nxt=True, prev=True):
                i = 2 * j + b
                if prev:
                    residual(i, b, j + b)
                if nxt:
                    mask(i + 1, 1 - b, 0)
                    mask(i + 1, 1 - b, 1)
                if this:
                    group(i, 0)
                    group(i, 1)
                if prev and not (isinstance(i, int) and i == 1):
                    ranks(i - 1)
                if nxt:
                    fill_zeros(i + 1, 1 - b, 0)
                    fill_zeros(i + 1, 1 - b, 1)
                    mask(i + 1, 1 - b, 2)
                if prev:
                    logits(i)
                if nxt:
                    fill_zeros(i + 1, 1 - b, 2)
                    mask(i + 1, 1 - b, 3)
                    fill_zeros(i + 1, 1 - b, 3)
                if not nxt:
                    pieces(0, (None, 0, 0), 0, 2)
                ahead = queries_follow(j, b, nxt)
                if ahead:
                    queries(2 * j + 2, 0)
                if prev:
                    picks(i)
                if this:
                    group(i, 2)
                if prev:
                    pick_weights(i)
                if not nxt:
                    pieces(0, (None, 0, 0), 2, 4)
                if ahead:
                    queries(2 * j + 3, 1)
                if this:
                    group(i, 3)
                if not nxt:
                    pieces(0, (None, 0, 0), 4, SPLIT_GU)
                if nxt:
                    row_max(i + 1, 1 - b)
                if prev:
                    take_counts(i)

            queries(0, 0)
            queries(1, 1)
            for n in range(KB):
                mask(0, 0, n)
                fill_zeros(0, 0, n)
            row_max(0, 0)
            dve.wait_ge(sem("pad_out"), 16 * (SLOT_TILES - NT + 1))
            dve.wait_ge(sem("in_bv"), 16)
            attention_step(0, 0, prev=False)
            attention_step(0, 1)
            with dve.Fori(1, NT // 2 - 1) as j:
                attention_step(j, 0)
                attention_step(j, 1)
            attention_step(NT // 2 - 1, 0)
            attention_step(NT // 2 - 1, 1, nxt=False)
            turned_rows(0)
            residual(NT, 0, NT // 2)
            ranks(NT - 1)

            def split_down(stage, m=0, n=SPLIT_DN):
                for c in range(m, n):
                    k = FC // SPLIT_DN
                    wait(dve, "dn_h", stage * SPLIT_DN + c + 1)
                    minus(dn_l[:, c * k:(c + 1) * k, :], dn_raw[:, c * k:(c + 1) * k, :],
                          dn_h[:, c * k:(c + 1) * k, :]).then_inc(sem("dn_l"), 1)

            def expert_tile(g, split=None, route=False):
                for f in range(2):
                    if route and f == 1:
                        logits(NT)
                    wait(dve, f"silu{f}", g + 1)
                    wait(dve, "up0" if f == 0 else "up_done", g + 1)
                    wait(dve, f"h_turned{f}", g)
                    dve.tensor_tensor(hid[:, f, :], bank[2 * f + 1][:], sil[:, f, :], ALU.mult).then_inc(sem(f"hid{f}"), 1)
                    if f == 0:
                        if route:
                            split_down(0, 2)
                        wait(dve, "added", g * 16)
                        wait(dve, "y_done", g)
                        wait(dve, "meta_next", g + 1)
                        dve.tensor_copy(meta[:].bitcast(I32), meta_next[:].bitcast(I32)).then_inc(sem("meta"), 1)
                        pieces(g, split, 0, 2)
                        hidden(g, 0)
                        pieces(g, split, 2, 3)
                pieces(g, split, 3, 4)
                if route:
                    picks(NT)
                hidden(g, 1)
                if route:
                    take_counts(NT)
                    pick_weights(NT)
                    ranks(NT)
                turned_rows(g + 1)
                pieces(g, split, 4, SPLIT_GU)

            def hidden(g, f):
                wait(dve, f"hT_h{f}", g + 1)
                minus(hT["l"][:, 4 * f:4 * f + 4, :], bank[4 + f][:].rearrange("p (c q) -> p c q", c=4),
                      hT["h"][:, 4 * f:4 * f + 4, :]).then_inc(sem(f"hT_l{f}"), 1)

            chain = [0]

            def then(ins):
                chain[0] += 1
                ins.then_inc(sem("placing"), 1)
                dve.wait_ge(sem("placing"), chain[0])

            def place_picks():
                then(dve.tensor_scalar(tiles_f[:], base[:], float(P - 1), None, ALU.add))
                then(dve.tensor_copy(cnt_i[:], tiles_f[:]))
                then(dve.tensor_scalar(tiles_i[:], cnt_i[:], P.bit_length() - 1, None, ALU.arith_shift_right))
                then(dve.tensor_scalar(tiles_f[:], tiles_i[:], 1.0, None, ALU.max))
                then(dve.memset(bnd[:, 0:1], 0.0))
                then(dve.memset(bnd[:, 1:2], float(NT)))
                for e in range(E):
                    then(dve.tensor_tensor(bnd[:, e + 2:e + 3], bnd[:, e + 1:e + 2], tiles_f[:, e:e + 1], ALU.add))
                then(dve.tensor_scalar(cut[:, 0, :], bnd[:, 0:E + 1], 1.0, None, ALU.add))
                then(dve.tensor_scalar(cut[:, 1, :], bnd[:, 1:E + 2], -1.0, None, ALU.add))
                then(dve.tensor_tensor(cut[:, 0, :], cut[:, 0, :], cut[:, 1, :], ALU.min))
                then(dve.memset(cut[:, 0, E:E + 1], 0.0))
                then(dve.tensor_copy(table[:, 0:E + 2], bnd[:]))
                then(dve.tensor_copy(table[:, 16:16 + E], cut[:, 0, 1:E + 1]))
                then(dve.tensor_scalar(off[:], bnd[:, 1:E + 1], float(P), -float(P * NT), ALU.mult, ALU.add))
                for k in range(2):
                    for e in range(E):
                        then(dve.tensor_scalar(place[:, :, e], routes[:, :, k * E + e], off[:, e:e + 1], None, ALU.mult))
                    then(dve.tensor_reduce(where[:], place[:], AX, ALU.add))
                    then(dve.tensor_tensor(wherek[:], where[:], routes[:, :, 2 * E + k], ALU.add))
                    then(dve.tensor_copy(pos_i[:, k, :], wherek[:]))
                dve.tensor_copy(bnd[:, 0:1], bnd[:, 0:1]).then_inc(sem("table"), 1)

            split_down(0, 0, 2)
            for g in range(UNPLACED):
                expert_tile(g, None, g == 0)
            place_picks()
            with dve.Fori(UNPLACED, EARLY) as g:
                expert_tile(g)
            expert_tile(EARLY, (None, 1, 1))
            with dve.Fori(EARLY + 1, NT) as g:
                expert_tile(g)
            with dve.Fori(0, E // 2) as j:
                for k in range(2):
                    e = 2 * j + k
                    first = dve.value_load(table[0:1, bass.ds(e + 1, 1)], min_val=NT, max_val=MAX_TILES)
                    end = dve.value_load(table[0:1, bass.ds(e + 2, 1)], min_val=NT, max_val=MAX_TILES)
                    when = dve.value_load(table[0:1, bass.ds(e + 16, 1)], min_val=0, max_val=MAX_TILES)
                    split_down(e + 1)
                    with dve.Fori(first, end) as g:
                        expert_tile(g, (when, k, e + 2))


_INS = ['x', 'adj', 'L0_gnn_W_q', 'L0_gnn_b_q', 'L0_gnn_W_k', 'L0_gnn_b_k', 'L0_gnn_W_v', 'L0_gnn_b_v',
        'L0_ffn_Wr', 'L0_ffn_Wg_s', 'L0_ffn_Wu_s', 'L0_ffn_Wd_s', 'L0_ffn_Wg', 'L0_ffn_Wu', 'L0_ffn_Wd']
_OUTS = [((2048, 512), 'float32')]


def kernel(**inputs):
    import numpy as _np
    import concourse.bacc as _bacc
    from concourse import mybir as _mybir
    from concourse.bass_utils import run_bass_kernel_spmd as _run

    nc = _bacc.Bacc("TRN2", target_bir_lowering=False, num_devices=1)
    arrays, args = {}, []
    for name in _INS:
        a = _np.ascontiguousarray(inputs[name])
        arrays[f"in_{name}_dram"] = a
        args.append(nc.dram_tensor(f"in_{name}_dram", a.shape, _mybir.dt.from_np(a.dtype), kind="ExternalInput").ap())
    for i, (shape, dtype) in enumerate(_OUTS):
        dt = _mybir.dt.from_np(_np.dtype(dtype))
        args.append(nc.dram_tensor(f"out_{i}_dram", shape, dt, kind="ExternalOutput").ap())
    gnn_moe(nc, *args)
    r = _run(nc, [arrays], core_ids=[0])
    got = tuple(r.results[0][f"out_{i}_dram"] for i in range(len(_OUTS)))
    return got[0]
```

```python
from contextlib import ExitStack

import concourse.bass as bass
from concourse import mybir

F32 = mybir.dt.float32
F32R = mybir.dt.float32r
I32 = mybir.dt.int32
U32 = mybir.dt.uint32
ALU = mybir.AluOpType
ACT = mybir.ActivationFunctionType
AX = mybir.AxisListType.X

P = 128
LN_EPS = 1e-5
MASKED = -10000.0


def gnn_moe(nc, x, adj, w_q, b_q, w_k, b_k, w_v, b_v, w_r, wg_s, wu_s, wd_s, wg, wu, wd, out):
    T, D = x.shape
    E, _, F = wg.shape
    NT = T // P
    DC = D // P
    FC = F // P
    KB = T // 512
    SCALE = 1.0 / float(D) ** 0.5
    LAST = 2
    FIRST = NT - LAST
    MAX_TILES = NT + 2 * T // P + E
    SLOT_TILES = MAX_TILES + 2 - FIRST
    ROW = D + 2
    assert D == 512 and F == 1024 and E == 8 and NT == 16

    acc = nc.dram_tensor("acc", [T + P, D], F32, kind="Internal").ap()
    tokens = nc.dram_tensor("tokens", [T, ROW], F32, kind="Internal").ap()
    slots = nc.dram_tensor("slots", [SLOT_TILES * P, ROW], F32, kind="Internal").ap()

    with ExitStack() as ctx:
        BASE = 16512

        def at(name, offset, shape, dtype=F32):
            return nc.alloc_sbuf_tensor_at(name, shape, dtype, offset=BASE + offset)

        K = 1024
        ctx.enter_context(nc.sbuf_tensor("arena", [P, 207 * K], mybir.dt.uint8))
        xnT = {"h": at("xnT_h", 0, [P, DC, T], F32R), "l": at("xnT_l", 32 * K, [P, DC, T], F32R)}
        v = {"h": at("v_h", 64 * K, [P, NT, D], F32R), "l": at("v_l", 96 * K, [P, NT, D], F32R)}
        A = {"h": at("A_h", 128 * K, [P, DC, D], F32R), "l": at("A_l", 136 * K, [P, DC, D], F32R)}
        yT = {"h": at("yT_h", 144 * K, [P, DC, 256], F32R), "l": at("yT_l", 148 * K, [P, DC, 256], F32R)}
        pT = {"h": at("pT_h", 152 * K, [P, 2, 512], F32R), "l": at("pT_l", 156 * K, [P, 2, 512], F32R)}
        adj_t = at("adj_t", 160 * K, [P, T])
        sc = at("sc", 168 * K, [P, 2, T])
        fill = at("fill", 184 * K, [P, 512])
        y_f = at("y_f", 186 * K, [P, 2, 256])
        x_t = at("x_t", 188 * K, [P, 2, D])
        x1 = at("x1", 192 * K, [P, D])
        x2T = at("x2T", 194 * K, [P, DC, P])
        x2row = at("x2row", 196 * K, [P, ROW])
        bv_row = at("bv_row", 198 * K + 64, [P, D])
        wk_raw = at("wk_raw", 168 * K, [P, DC, D])
        wq_raw = at("wq_raw", 176 * K, [P, DC, D])
        wv_raw = at("wv_raw", 160 * K, [P, DC, D])
        wq = {"h": at("wq_h", 64 * K, [P, DC, D], F32R), "l": at("wq_l", 72 * K, [P, DC, D], F32R)}
        wk = {"h": at("wk_h", 80 * K, [P, DC, D], F32R), "l": at("wk_l", 88 * K, [P, DC, D], F32R)}
        wvT = {"h": at("wvT_h", 144 * K, [P, DC, D], F32R), "l": at("wvT_l", 152 * K, [P, DC, D], F32R)}
        xn = at("xn", 184 * K, [P, 2, D])
        xT1 = {"h": at("xT1_h", 160 * K, [P, 2, DC, P], F32R), "l": at("xT1_l", 164 * K, [P, 2, DC, P], F32R)}
        c2_rep = at("c2_rep", 194 * K, [P, D])
        before = at("before", 196 * K, [P, P])
        ones = at("ones", 196 * K + 512, [P, P])
        spent = at("spent", 196 * K, [P, D])
        bk_rep = at("bk_rep", 192 * K, [P, DC, P])
        gu_h = [[at(f"gu{s}{m}_h", 64 * K * s + 32 * K * m, [P, DC, F], F32R) for m in range(2)] for s in range(2)]
        gu_l = [[at(f"gu{s}{m}_l", 64 * K * s + 32 * K * m + 16 * K, [P, DC, F], F32R) for m in range(2)] for s in range(2)]
        gu_raw = [[at(f"gu{s}{m}_raw", 64 * K * s + 32 * K * m + 16 * K, [P, DC, F]) for m in range(2)] for s in range(2)]
        gate_s_raw = at("gate_s_raw", 128 * K, [P, DC, F])
        dn_h = at("dn_h", 128 * K, [P, FC, D], F32R)
        dn_l = at("dn_l", 144 * K, [P, FC, D], F32R)
        dn_raw = at("dn_raw", 160 * K, [P, FC, D])
        e_x = at("e_x", 176 * K, [P, ROW])
        e_xT = {"h": at("e_xT_h", 179 * K, [P, DC, P], F32R), "l": at("e_xT_l", 181 * K, [P, DC, P], F32R)}
        hid = at("hid", 183 * K, [P, 2, 512])
        sil = at("sil", 187 * K, [P, 2, 512])
        hT = {"h": at("hT_h", 191 * K, [P, FC, P], F32R), "l": at("hT_l", 195 * K, [P, FC, P], F32R)}
        y = at("y", 199 * K, [P, D])
        send = at("send", 64 * K, [P, 4, ROW])
        padrow = at("padrow", 80 * K, [P, ROW])
        small = [201 * K + 64]

        def keep(name, shape, dtype=F32):
            n = 4
            for k in shape[1:]:
                n *= k
            t = at(name, small[0], shape, dtype)
            small[0] += -(-n // 32) * 32
            assert small[0] <= 207 * K
            return t

        ident = keep("ident", [P, P])
        before_r = keep("before_r", [P, P], F32R)
        ones_r = keep("ones_r", [P, P], F32R)
        w_r_sb = keep("w_r_sb", [P, DC, E])
        bqk = keep("bqk", [P, 2, DC])
        c1 = keep("c1", [P, DC])
        bb = keep("bb", [P, 1])
        s_q = keep("s_q", [P, NT])
        iota8 = keep("iota8", [P, E])
        stat = keep("stat", [P, 6])
        mv = keep("mv", [P, 2, 2])
        var_e = keep("var_e", [P, 2])
        neg_half = keep("neg_half", [P, 1])
        rstd = keep("rstd", [P, 2])
        mx4 = keep("mx4", [P, KB])
        nmx = keep("nmx", [P, 2])
        den = keep("den", [P, 2])
        rden = keep("rden", [P, 1])
        lg = keep("lg", [P, E])
        tok = keep("tok", [P, NT], I32)
        nlm = keep("nlm", [P, 1])
        lex = keep("lex", [P, E])
        lsum = keep("lsum", [P, 1])
        lrs = keep("lrs", [P, 1])
        rw = keep("rw", [P, E])
        top = keep("top", [P, 8])
        topi = keep("topi", [P, 8], U32)
        topf = keep("topf", [P, 2])
        tdiff = keep("tdiff", [P, 1])
        tex = keep("tex", [P, 1])
        tsum = keep("tsum", [P, 1])
        route = keep("route", [P, 2 * E + 4])
        routes = keep("routes", [P, NT, 2 * E + 4])
        both = keep("both", [P, E], F32R)
        counts = keep("counts", [P, 2 * E])
        rank = keep("rank", [P, E])
        base = keep("base", [P, E])
        rsel = keep("rsel", [P, E])
        place = keep("place", [P, NT, E])
        where = keep("where", [P, NT])
        wherek = keep("wherek", [P, NT])
        pos_i = keep("pos_i", [P, 2, NT], I32)
        idx = keep("idx", [P, 4], I32)
        cnt_i = keep("cnt_i", [P, E], I32)
        tiles_i = keep("tiles_i", [P, E], I32)
        tiles_f = keep("tiles_f", [P, E])
        bnd = keep("bnd", [P, E + 3])
        off = keep("off", [P, E])
        cut = keep("cut", [P, 2, E + 1])
        table = keep("table", [P, 32], I32)
        meta_next = keep("meta_next", [P, 2])
        meta = keep("meta", [P, 2])

        bank = [ctx.enter_context(nc.psum_tensor(f"bank{n}", [P, 512], F32)) for n in range(8)]
        sems = {}

        def sem(name):
            if name not in sems:
                sems[name] = ctx.enter_context(nc.semaphore(name))
            return sems[name]

        def wait(eng, name, value):
            if isinstance(value, int) and value <= 0:
                return
            eng.wait_ge(sem(name), value)

        def wait_apart(eng, name, value):
            wait(eng, name, value)
            if not isinstance(value, int):
                eng.sem_inc(sem(f"waits_{eng.engine.name}"), 1)

        def rows(a, t):
            return a[bass.ds(t * P, P), :]

        PASSES = (("h", "h"), ("h", "l"), ("l", "h"))

        def product(pe, o, lhs, rhs, chunks, first=True, last=True):
            n = 0
            for c in chunks:
                for a, b in PASSES:
                    n += 1
                    mm = pe.matmul(o, lhs(a, c), rhs(b, c), start=first and n == 1,
                                   stop=last and n == 3 * len(chunks))
            return mm

        block = ctx.enter_context(nc.Block())

        SPLIT_GU = 2 * DC
        SPLIT_DN = 4
        UNPLACED = 2
        EARLY = FIRST - 2

        def queries_follow(j, b):
            return b == 0 and (not isinstance(j, int) or j + 1 < NT // 2)

        @block.sync
        def _(sp):
            def load_x(t, b):
                sp.dma_start(x_t[:, b, :], rows(x, t)).then_inc(sem(f"x_in{b}"), 16)

            sp.dma_start(bqk[:, 0, :], b_q.rearrange("(p c) -> p c", c=DC)).then_inc(sem("in_b"), 16)
            sp.dma_start(bqk[:, 1, :], b_k.rearrange("(p c) -> p c", c=DC)).then_inc(sem("in_b"), 16)
            sp.dma_start(wq_raw[:], w_q.rearrange("(p c) n -> p c n", c=DC)).then_inc(sem("in_wq"), 16)
            sp.dma_start(wk_raw[:], w_k.rearrange("(p c) n -> p c n", c=DC)).then_inc(sem("in_wk"), 16)
            sp.dma_start(wv_raw[:], w_v.rearrange("(c p) n -> p c n", p=P)).then_inc(sem("in_wv"), 16)
            load_x(0, 0)
            load_x(1, 1)
            sp.dma_start(bv_row[:], b_v.rearrange("(a n) -> a n", a=1).broadcast_to([P, D])).then_inc(sem("in_bv"), 16)
            sp.dma_start(w_r_sb[:], w_r.rearrange("(c p) e -> p c e", p=P)).then_inc(sem("in_wr"), 16)

            with sp.Fori(1, NT // 2) as j:
                for b in range(2):
                    wait(sp, "ln1_done", 2 * j + b - 1)
                    load_x(2 * j + b, b)
            wait(sp, "ln1_done", NT)
            wait(sp, "v_ps", NT)
            wait(sp, "xnT_h", NT)
            wait(sp, "xnT_l", NT)
            sp.dma_start(adj_t[:], rows(adj, 0)).then_inc(sem("adj_in"), 16)

            def fetch(i, b):
                if not isinstance(i, int) or i < NT - 1:
                    wait(sp, "scored", 4 * i + 4)
                    sp.dma_start(adj_t[:], rows(adj, i + 1)).then_inc(sem("adj_in"), 16)
                wait(sp, "x1_done", i - 1)
                sp.dma_start(x_t[:, b, :], rows(x, i)).then_inc(sem(f"xr_in{b}"), 16)

            def store(i):
                wait(sp, "x1_done", i + 1)
                sp.dma_start(rows(acc, i), x1[:]).then_inc(sem("x1_out"), 16)
                wait(sp, "x2_done", i + 1)
                wait(sp, "x2meta", i + 1)
                sp.dma_start(rows(tokens, i), x2row[:]).then_inc(sem("x2_out"), 16)

            fetch(0, 0)
            fetch(1, 1)
            store(0)
            with sp.Fori(1, NT // 2 - 1) as j:
                for b in range(2):
                    fetch(2 * j + b, b)
                    store(2 * j + b - 1)
            fetch(NT - 2, 0)
            store(NT - 3)
            wait(sp, "y_ps", NT)
            sp.dma_start(gate_s_raw[:], wg_s.rearrange("(c p) f -> p c f", p=P)).then_inc(sem("gate_s_in"), 16)
            fetch(NT - 1, 1)
            wait(sp, "scores", 4 * NT)
            sp.dma_start(gu_raw[0][1][:], wu_s.rearrange("(c p) f -> p c f", p=P)).then_inc(sem("gu_in0"), 16)
            wait(sp, "scored", 4 * NT)
            wait(sp, "p_turned", 4 * (NT - 1))
            sp.dma_start(dn_raw[:], wd_s.rearrange("(c p) d -> p c d", p=P)).then_inc(sem("dn_in"), 16)
            store(NT - 2)
            wait(sp, "p_turned", 4 * NT)
            sp.dma_start(e_x[:], rows(tokens, 0)).then_inc(sem("e_x_in"), 16)
            store(NT - 1)
            wait(sp, "x2_out", 16 * NT)

            def load_send(t, k):
                sp.dma_start(send[:, k, :], rows(tokens, t)).then_inc(sem(f"send_in{k}"), 16)
            for k in range(4):
                load_send(k // 2, k)
            sp.wait_ge(sem("pad"), 2)
            sp.dma_start(acc[T:T + P, :], padrow[:, 0:D]).then_inc(sem("pad_out"), 16)
            wait(sp, "table", 1)
            with sp.Fori(0, E) as e:
                end = sp.value_load(table[0:1, bass.ds(e + 2, 1)], min_val=FIRST + 1, max_val=MAX_TILES)
                sp.dma_start(rows(slots, end - FIRST - 1), padrow[:]).then_inc(sem("pad_out"), 16)
            routed_end = sp.value_load(table[0:1, E + 1:E + 2], min_val=FIRST, max_val=MAX_TILES - LAST)
            for t in range(LAST, LAST + 2):
                sp.dma_start(rows(slots, routed_end - FIRST + t), padrow[:]).then_inc(sem("pad_out"), 16)
            sp.dma_start(slots[bass.ds((routed_end - FIRST) * P, LAST * P), :], tokens[FIRST * P:T, :]
                         ).then_inc(sem("last_in_slots"), 16)
            with sp.Fori(1, NT // 2) as j:
                for k in range(4):
                    sp.wait_ge(sem(f"sent{k}"), j * 16)
                    load_send(2 * j + k // 2, k)
            for k in range(4):
                sp.wait_ge(sem(f"sent{k}"), NT // 2 * 16)
            sp.wait_ge(sem("pad_out"), 16 * (E + 3))

            def load_gate_up(s, gate, up, after=0):
                for m, w in enumerate((gate, up)):
                    if m == 1:
                        wait(sp, "added", after)
                    sp.dma_start(gu_raw[s][m][:], w.rearrange("(c p) f -> p c f", p=P)).then_inc(sem(f"gu_in{s}"), 16)

            def load_down(e, w):
                wait(sp, "dn_l", SPLIT_DN * (e + 1))
                sp.dma_start(dn_raw[:], w.rearrange("(c p) d -> p c d", p=P)).then_inc(sem("dn_in"), 16)

            def of_expert(w, e):
                return w[bass.ds(e, 1), :, :].rearrange("e f d -> (e f) d")

            load_gate_up(1, of_expert(wg, 0), of_expert(wu, 0), (FIRST - 3) * 16)
            wait(sp, "added", (FIRST - 2) * 16)
            load_down(0, of_expert(wd, 0))
            wait(sp, "up_done", FIRST)
            load_gate_up(0, of_expert(wg, 1), of_expert(wu, 1))
            load_down(1, of_expert(wd, 1))
            with sp.Fori(1, E // 2) as j:
                for s in range(2):
                    e = 2 * j + s
                    end = sp.value_load(table[0:1, bass.ds(e, 1)], min_val=FIRST, max_val=MAX_TILES)
                    wait(sp, "up_done", end)
                    load_gate_up(1 - s, of_expert(wg, e), of_expert(wu, e))
                    load_down(e, of_expert(wd, e))
            end = sp.value_load(table[0:1, E:E + 1], min_val=FIRST, max_val=MAX_TILES)
            wait(sp, "up_done", end)
            load_gate_up(1, wg_s, wu_s)
            load_down(E, wd_s)
            wait(sp, "added", routed_end * 16)
            sp.dma_start(out[0:FIRST * P, :], acc[0:FIRST * P, :]).then_inc(sem("out"), 16)
            n_tiles = sp.value_load(table[0:1, E + 2:E + 3], min_val=FIRST, max_val=MAX_TILES)
            wait(sp, "e_x_in", n_tiles * 16 + 32)
            wait(sp, "added", n_tiles * 16)
            sp.dma_start(out[FIRST * P:T, :], acc[FIRST * P:T, :]).then_inc(sem("out"), 16)
            sp.wait_ge(sem("out"), 32)

        @block.gpsimd
        def _(pool):
            pool.memset(ident[:], 0.0).then_inc(sem("pz"), 1)
            pool.memset(before[:], 1.0).then_inc(sem("pz"), 1)
            pool.memset(ones[:], 1.0).then_inc(sem("consts"), 1)
            pool.memset(neg_half[:], -0.5).then_inc(sem("consts"), 1)
            pool.memset(base[:], 0.0).then_inc(sem("consts"), 1)
            pool.iota(iota8[:], pattern=[[1, E]], base=0, channel_multiplier=0,
                      allow_small_or_imprecise_dtypes=True).then_inc(sem("consts"), 1)
            pool.iota(tok[:], pattern=[[P, NT]], base=0, channel_multiplier=1).then_inc(sem("tok"), 1)
            pool.wait_ge(sem("pz"), 2)
            pool.affine_select(out=ident[:], in_=ident[:], compare_op=ALU.not_equal, fill=1.0, base=0,
                               pattern=[[-1, P]], channel_multiplier=1).then_inc(sem("consts"), 1)
            pool.affine_select(out=before[:], in_=before[:], compare_op=ALU.is_gt, fill=0.0, base=0,
                               pattern=[[1, P]], channel_multiplier=-1).then_inc(sem("consts"), 1)

            def power(n, b):
                wait(pool, "var", n)
                pool.tensor_tensor(rstd[:, b:b + 1], var_e[:, b:b + 1], neg_half[:], ALU.pow).then_inc(sem("rstd"), 1)

            pool.wait_ge(sem("consts"), 6)
            power(1, 0)
            power(2, 1)
            with pool.Fori(0, NT // 2 - 1) as j:
                for b in range(2):
                    t = 2 * j + b
                    pool.wait_ge(sem("xT1_l"), t + 1)
                    pool.tensor_copy(xnT["l"][:, :, bass.ds(t * P, P)],
                                     xT1["l"][:, b, :, :].bitcast(F32)).then_inc(sem("xnT_l"), 1)
                    power(t + 3, b)
            for t in range(NT - 2, NT):
                for b in [t % 2]:
                    pool.wait_ge(sem("xT1_l"), t + 1)
                    pool.tensor_copy(xnT["l"][:, :, bass.ds(t * P, P)],
                                     xT1["l"][:, b, :, :].bitcast(F32)).then_inc(sem("xnT_l"), 1)
            pool.wait_ge(sem("tok"), 1)
            pool.memset(x2row[:, D:D + 1], 1.0).then_inc(sem("x2_weight"), 1)

            def label(t, b):
                wait(pool, "x2_out", t * 16)
                pool.tensor_copy(x2row[:, D + 1:ROW].bitcast(I32), tok[:, bass.ds(t, 1)]).then_inc(sem("x2meta"), 1)
                power(NT + t + 1, b)

            label(0, 0)
            label(1, 1)
            with pool.Fori(1, NT // 2) as j:
                label(2 * j, 0)
                label(2 * j + 1, 1)

            def add(g):
                wait_apart(pool, "y_done", g + 1)
                pool.indirect_dma_start(acc, bass.IndirectOffsetOnAxis(ap=meta[:, 1:2].bitcast(I32), axis=0),
                                        y[:], None, compute_op=ALU.add).then_inc(sem("added"), 16)
                pool.wait_ge(sem("added"), g * 16 + 16)

            pool.wait_ge(sem("attended"), 4 * NT)
            pool.memset(padrow[:, 0:D + 1], 0.0).then_inc(sem("pad"), 1)
            pool.iota(padrow[:, D + 1:ROW].bitcast(I32), pattern=[[0, 1]], base=T, channel_multiplier=1).then_inc(sem("pad"), 1)
            with pool.Fori(0, UNPLACED) as g:
                add(g)
            pool.wait_ge(sem("table"), 1)
            pool.wait_ge(sem("pad_out"), 16 * (E + 3))
            with pool.Fori(0, NT // 2) as j:
                add(j + UNPLACED)
                for k in range(4):
                    n = 4 * j + k
                    t = 2 * j + k // 2
                    pool.wait_ge(sem(f"send_in{k}"), j * 16 + 16)
                    pool.tensor_copy(send[:, k, D:D + 1], routes[:, bass.ds(t, 1), 2 * E + 2 + k % 2]).then_inc(sem("addressed"), 1)
                    pool.tensor_copy(idx[:, k:k + 1], pos_i[:, k % 2, bass.ds(t, 1)]).then_inc(sem("addressed"), 1)
                    wait_apart(pool, "addressed", 2 * n + 2)
                    pool.indirect_dma_start(slots, bass.IndirectOffsetOnAxis(ap=idx[:, k:k + 1], axis=0),
                                            send[:, k, :], None).then_inc(sem(f"sent{k}"), 16)
            n_tiles = pool.value_load(table[0:1, E + 2:E + 3], min_val=FIRST, max_val=MAX_TILES)
            with pool.Fori(NT // 2 + UNPLACED, n_tiles) as g:
                add(g)

        @block.tensor
        def _(pe):
            pe.wait_ge(sem("consts"), 6)
            pe.wait_ge(sem("bk_rep"), DC)
            pe.wait_ge(sem("in_wq"), 16)
            for o in range(DC):
                mm = pe.matmul(bank[6][:], bk_rep[:, o, :], wq_raw[:, o, :], start=o == 0, stop=o == DC - 1)
            mm.then_inc(sem("c2_ps"), 1)
            pe.wait_ge(sem("in_wv"), 16)
            for c in range(DC):
                for o in range(DC):
                    mm = pe.transpose(bank[c][:, o * P:(o + 1) * P], wv_raw[:, o, c * P:(c + 1) * P], ident[:])
                mm.then_inc(sem("wv_turned"), 1)
            pe.wait_ge(sem("wqk_l"), 2)

            def A_chunk(c):
                product(pe, bank[4 + c][:], lambda a, o: wq[a][:, o, c * P:(c + 1) * P],
                        lambda b, o: wk[b][:, o, :], range(DC)).then_inc(sem("A_ps"), 1)

            def before_attention(t, b, this, prev):
                if this:
                    wait(pe, "ln1_done", t + 1)
                    wait(pe, "xT1_l", t - 1)
                    for c in range(DC):
                        mm = pe.transpose(bank[b][:, c * P:(c + 1) * P], xn[:, b, c * P:(c + 1) * P], ident[:])
                    mm.then_inc(sem("xn_turned"), 1)
                if prev:
                    wait(pe, "xT1_l", t)
                    wait(pe, "v_l", t - 2)
                    product(pe, bank[3 - b][:], lambda a, c: xT1[a][:, 1 - b, c, :],
                            lambda b_, c: wvT[b_][:, c, :], range(DC)).then_inc(sem("v_ps"), 1)

            A_chunk(0)
            A_chunk(1)
            pe.wait_ge(sem("wvT_l"), DC)
            before_attention(0, 0, True, False)
            pe.wait_ge(sem("c2_done"), 1)
            A_chunk(2)
            A_chunk(3)
            before_attention(1, 1, True, True)
            pe.wait_ge(sem("in_b"), 32)
            pe.wait_ge(sem("A_done"), 1)
            for c in range(DC + 1):
                for o in range(DC):
                    lhs = wk_raw[:, o, c * P:(c + 1) * P] if c < DC else bk_rep[:, o, :]
                    mm = pe.matmul(bank[4][:, 2 * c:2 * c + 2], lhs, bqk[:, :, o], start=o == 0, stop=o == DC - 1)
                if c == 1:
                    before_attention(2, 0, True, True)
            mm.then_inc(sem("biases"), 1)
            before_attention(3, 1, True, True)
            with pe.Fori(2, NT // 2) as j:
                before_attention(2 * j, 0, True, True)
                before_attention(2 * j + 1, 1, True, True)
            def queries(j, half):
                for c in range(2):
                    m = 2 * half + c
                    mm = product(pe, bank[7][:, c * 256:(c + 1) * 256], lambda a, d: A[a][:, d, m * P:(m + 1) * P],
                                 lambda b, d: xnT[b][:, d, bass.ds(j * 256, 256)], range(DC))
                mm.then_inc(sem("y_ps"), 1)

            def scores(i, b, n):
                wait(pe, "scored", 4 * (i - 1) + n + 1)
                product(pe, bank[n][:], lambda a, c: yT[a][:, c, b * P:(b + 1) * P],
                        lambda b_, c: xnT[b_][:, c, n * 512:(n + 1) * 512], range(DC)).then_inc(sem("scores"), 1)

            def turn(i, b, g):
                wait(pe, "exp_done", i + 1)
                wait(pe, "pT_l", 4 * i + g - 1)
                for c in range(4):
                    k = 4 * g + c
                    mm = pe.transpose(bank[4 + g % 2][:, c * P:(c + 1) * P], sc[:, b, k * P:(k + 1) * P], ident[:])
                mm.then_inc(sem("p_turned"), 1)

            def attend(i, g):
                wait(pe, "pT_l", 4 * i + g + 1)
                if g == 0:
                    wait(pe, "o_done", i)
                product(pe, bank[6][:], lambda a, c: pT[a][:, g % 2, c * P:(c + 1) * P],
                        lambda b, c: v[b][:, 4 * g + c, :], range(4), first=g == 0, last=g == 3
                        ).then_inc(sem("attended"), 1)

            def turn_normalised(i):
                wait(pe, "x2_done", i)
                wait(pe, "counts_read", i - 1)
                for c in range(DC):
                    mm = pe.transpose(bank[7][:, c * P:(c + 1) * P], x2row[:, c * P:(c + 1) * P], ident[:])
                mm.then_inc(sem("x2_turned"), 1)

            def route_logits(i):
                wait(pe, "x2T_done", i)
                for c in range(DC):
                    mm = pe.matmul(bank[7][:, 0:E], x2T[:, c, :], w_r_sb[:, c, :], start=c == 0, stop=c == DC - 1)
                mm.then_inc(sem("logits"), 1)

            def count_picks(i):
                wait(pe, "logits_read", i)
                wait(pe, "picked", i)
                pe.matmul(bank[7][:, 0:E], before_r[:], both[:], start=True, stop=True)
                pe.matmul(bank[7][:, E:2 * E], ones_r[:], both[:], start=True, stop=True).then_inc(sem("counted"), 1)

            def attention_step(j, b, last=False, prev=True):
                i = 2 * j + b
                if not last:
                    if b == 1:
                        wait(pe, "yT_l", 2 * j + 4)
                    scores(i + 1, 1 - b, 0)
                    scores(i + 1, 1 - b, 1)
                turn(i, b, 0)
                turn(i, b, 1)
                if last:
                    attend(i, 0)
                    turn_normalised(i)
                    turn(i, b, 2)
                    attend(i, 1)
                    route_logits(i)
                    turn(i, b, 3)
                    attend(i, 2)
                    attend(i, 3)
                    count_picks(i)
                    return
                if prev:
                    turn_normalised(i)
                scores(i + 1, 1 - b, 2)
                if prev:
                    route_logits(i)
                scores(i + 1, 1 - b, 3)
                ahead = queries_follow(j, b)
                if ahead:
                    if prev:
                        wait(pe, "logits_read", i)
                    queries(j + 1, 0)
                attend(i, 0)
                turn(i, b, 2)
                attend(i, 1)
                if ahead:
                    wait(pe, "yT_f", 2 * j + 3)
                    queries(j + 1, 1)
                turn(i, b, 3)
                attend(i, 2)
                attend(i, 3)
                if prev:
                    if ahead:
                        wait(pe, "yT_f", 2 * j + 4)
                    count_picks(i)

            def turn_rows(g):
                wait(pe, "e_x_in", g * 16 + 16)
                wait(pe, "e_xT_l", g)
                for c in range(DC):
                    mm = pe.transpose(bank[7][:, c * P:(c + 1) * P], e_x[:, c * P:(c + 1) * P], ident[:])
                mm.then_inc(sem("x_turned"), 1)

            pe.wait_ge(sem("xnT_h"), 2)
            pe.wait_ge(sem("xnT_l"), 2)
            pe.wait_ge(sem("A_done"), DC)
            queries(0, 0)
            before_attention(NT, 0, False, True)
            pe.wait_ge(sem("xnT_h"), NT)
            pe.wait_ge(sem("xnT_l"), NT)
            pe.wait_ge(sem("v_l"), NT - 1)
            pe.wait_ge(sem("c1_done"), 2)
            pe.wait_ge(sem("triangle"), 2)
            pe.wait_ge(sem("yT_f"), 1)
            queries(0, 1)
            pe.wait_ge(sem("yT_l"), 2)
            for n in range(KB):
                if n == 2:
                    pe.wait_ge(sem("v_l"), NT)
                scores(0, 0, n)
            attention_step(0, 0, prev=False)
            attention_step(0, 1)
            with pe.Fori(1, NT // 2 - 1) as j:
                attention_step(j, 0)
                attention_step(j, 1)
            attention_step(NT // 2 - 1, 0)
            attention_step(NT // 2 - 1, 1, last=True)
            wait(pe, "counts_read", NT - 1)
            turn_rows(0)

            def expert_tile(g, s, downs, route=False):
                def project(m, f, read):
                    wait(pe, read, g)
                    n = 2 * f + m
                    return product(pe, bank[n][:], lambda a, c: e_xT[a][:, c, :],
                                   lambda b, c: (gu_h if b == "h" else gu_l)[s][m][:, c, f * 512:(f + 1) * 512], range(DC))

                def turn_hidden(f):
                    wait(pe, f"hid{f}", g + 1)
                    wait(pe, f"hT_l{f}", g)
                    for c in range(4):
                        mm = pe.transpose(bank[4 + f][:, c * P:(c + 1) * P], hid[:, f, c * P:(c + 1) * P], ident[:])
                    mm.then_inc(sem(f"h_turned{f}"), 1)

                def down(chunks):
                    return product(pe, bank[6][:], lambda a, c: hT[a][:, c, :],
                                   lambda b, c: (dn_h if b == "h" else dn_l)[:, c, :], chunks,
                                   first=chunks[0] == 0, last=chunks[-1] == FC - 1)

                wait(pe, "e_xT_l", g + 1)
                project(0, 0, "silu0").then_inc(sem("gate0"), 1)
                if route:
                    wait(pe, "gu_l", SPLIT_GU)
                project(1, 0, "hid0").then_inc(sem("up0"), 1)
                if route:
                    turn_normalised(NT)
                project(0, 1, "silu1").then_inc(sem("gate1"), 1)
                if route:
                    route_logits(NT)
                turn_hidden(0)
                project(1, 1, "hid1").then_inc(sem("up_done"), 1)
                wait(pe, "hT_l0", g + 1)
                wait(pe, "y_done", g)
                wait(pe, "dn_l", downs)
                down(range(0, 2))
                turn_hidden(1)
                down(range(2, 4))
                if route:
                    count_picks(NT)
                    wait(pe, "counts_read", NT)
                turn_rows(g + 1)
                wait(pe, "hT_l1", g + 1)
                down(range(4, FC)).then_inc(sem("down_done"), 1)

            pe.wait_ge(sem("gu_l"), DC)
            expert_tile(0, 0, SPLIT_DN, True)
            with pe.Fori(1, FIRST) as g:
                expert_tile(g, 0, SPLIT_DN)
            pe.wait_ge(sem("table"), 1)

            def stage(e, k):
                first = pe.value_load(table[0:1, bass.ds(e + 1, 1)], min_val=FIRST, max_val=MAX_TILES)
                end = pe.value_load(table[0:1, bass.ds(e + 2, 1)], min_val=FIRST, max_val=MAX_TILES)
                wait_apart(pe, "gu_l", e * SPLIT_GU + 2 * SPLIT_GU)
                with pe.Fori(first, end) as g:
                    expert_tile(g, 1 - k, e * SPLIT_DN + 2 * SPLIT_DN)

            with pe.Fori(0, E // 2) as j:
                for k in range(2):
                    stage(2 * j + k, k)
            stage(E, 0)

        @block.scalar
        def _(act):
            def copy(o, i, scale=None):
                return act.activation(o, i, ACT.Copy) if scale is None else act.activation(o, i, ACT.Copy, scale=scale)

            act.wait_ge(sem("in_wq"), 16)
            copy(wq["h"][:], wq_raw[:]).then_inc(sem("wqk_h"), 1)
            act.wait_ge(sem("in_wk"), 16)
            copy(wk["h"][:], wk_raw[:]).then_inc(sem("wqk_h"), 1)
            for c in range(DC):
                wait(act, "wv_turned", c + 1)
                copy(wvT["h"][:, c, :], bank[c][:]).then_inc(sem("wvT_h"), 1)

            def A_chunks(m, n):
                for c in range(m, n):
                    wait(act, "A_ps", c + 1)
                    copy(A["h"][:, c, :], bank[4 + c][:]).then_inc(sem("A_h"), 1)

            A_chunks(0, 2)
            act.wait_ge(sem("wv_turned"), DC)

            def before_attention(t, b, this, prev):
                if this:
                    wait(act, "xn_turned", t + 1)
                    wait(act, "v_ps", t - 1)
                    wait(act, "xnT_h", t - 1)
                    wait(act, "xT1_l", t - 1)
                    copy(xT1["h"][:, b, :, :], bank[b][:].rearrange("p (c q) -> p c q", c=DC)).then_inc(sem("xT1_h"), 1)
                    wait(act, "xT1_h", t + 1)
                    copy(xnT["h"][:, :, bass.ds(t * P, P)], xT1["h"][:, b, :, :].bitcast(F32)).then_inc(sem("xnT_h"), 1)
                if prev:
                    wait(act, "v_ps", t)
                    copy(v["h"][:, bass.ds(t - 1, 1), :], bank[3 - b][:].rearrange("p (a n) -> p a n", a=1)).then_inc(sem("v_h"), 1)

            before_attention(0, 0, True, False)
            A_chunks(2, DC)
            before_attention(1, 1, True, True)
            before_attention(2, 0, True, True)
            before_attention(3, 1, True, True)
            with act.Fori(2, NT // 2) as j:
                before_attention(2 * j, 0, True, True)
                before_attention(2 * j + 1, 1, True, True)
            before_attention(NT, 0, False, True)

            def pieces(g, split, n, m):
                if split is None:
                    return
                when, s, filling = split
                if when is not None:
                    with act.If(g == when):
                        pieces(g, (None, s, filling), n, m)
                    return
                shared = isinstance(filling, int) and filling == 0
                if n == 0 and shared:
                    wait(act, "gate_s_in", 16)
                    wait(act, "scores", 4 * NT)
                elif not shared or m > DC:
                    wait(act, f"gu_in{s}", filling * 32 + (16 if s == 0 else 0))
                for k in range(n, m):
                    raw = gate_s_raw if shared and k < DC else gu_raw[s][k // DC]
                    copy(gu_h[s][k // DC][:, k % DC, :], raw[:, k % DC, :]).then_inc(sem("gu_h"), 1)

            def turned_rows(g):
                wait(act, "x_turned", g + 1)
                wait(act, "up_done", g)
                wait(act, "e_xT_l", g)
                copy(e_xT["h"][:], bank[7][:].rearrange("p (c q) -> p c q", c=DC)).then_inc(sem("e_xT_h"), 1)

            def queries(n, half):
                wait(act, "yT_f", n + 1)
                copy(yT["h"][:, 2 * half:2 * half + 2, :], y_f[:]).then_inc(sem("yT_h"), 1)

            def probabilities(i, b):
                wait(act, "nmx_done", i + 1)
                act.activation(sc[:, b, :], sc[:, b, :], ACT.Exp, bias=nmx[:, b:b + 1],
                               accum_out=den[:, b:b + 1]).then_inc(sem("exp_done"), 1)

            def group(i, g):
                n = 4 * i + g
                wait(act, "p_turned", n + 1)
                wait(act, "attended", n - 1)
                wait(act, "pT_l", n - 1)
                copy(pT["h"][:, g % 2, :], bank[4 + g % 2][:]).then_inc(sem("pT_h"), 1)

            def keep_turned(i):
                wait(act, "x2_turned", i)
                wait(act, "logits", i - 1)
                copy(x2T[:], bank[7][:].rearrange("p (c q) -> p c q", c=DC)).then_inc(sem("x2T_done"), 1)

            def router_exp(i):
                wait(act, "nlm_done", i)
                act.activation(lex[:], lg[:], ACT.Exp, bias=nlm[:], accum_out=lsum[:]).then_inc(sem("lex_done"), 1)

            def pick_exp(i):
                wait(act, "tdiff_done", i)
                act.activation(tex[:], tdiff[:], ACT.Exp).then_inc(sem("tex_done"), 1)

            def attention_step(j, b, last=False, prev=True, split=False):
                i = 2 * j + b
                group(i, 0)
                group(i, 1)
                if last:
                    pieces(0, (None, 0, 0), 2, 4)
                    keep_turned(i)
                    group(i, 2)
                    router_exp(i)
                    group(i, 3)
                    pick_exp(i)
                    pieces(0, (None, 0, 0), 4, SPLIT_GU)
                    return
                if prev:
                    keep_turned(i)
                    router_exp(i)
                ahead = queries_follow(j, b)
                if ahead:
                    queries(2 * j + 2, 0)
                group(i, 2)
                if prev:
                    pick_exp(i)
                if ahead:
                    queries(2 * j + 3, 1)
                if split:
                    pieces(0, (None, 0, 0), 0, 2)
                group(i, 3)
                probabilities(i + 1, 1 - b)

            act.wait_ge(sem("v_ps"), NT)
            queries(0, 0)
            queries(1, 1)
            probabilities(0, 0)
            attention_step(0, 0, prev=False)
            attention_step(0, 1)
            with act.Fori(1, NT // 2 - 1) as j:
                attention_step(j, 0)
                attention_step(j, 1)
            attention_step(NT // 2 - 1, 0, split=True)
            attention_step(NT // 2 - 1, 1, last=True)
            turned_rows(0)
            wait(act, "meta_next", 1)
            act.dma_start(e_x[:], rows(tokens, 1)).then_inc(sem("e_x_in"), 16)

            def split_down(stage, first, m=0, n=SPLIT_DN):
                wait(act, "dn_in", stage * 16 + 16)
                wait(act, "down_done", first)
                for c in range(m, n):
                    k = FC // SPLIT_DN
                    copy(dn_h[:, c * k:(c + 1) * k, :], dn_raw[:, c * k:(c + 1) * k, :]).then_inc(sem("dn_h"), 1)

            def expert_tile(g, source, row, split=None, route=False, down=None):
                for f in range(2):
                    wait(act, f"gate{f}", g + 1)
                    wait(act, f"hid{f}", g)
                    if route:
                        wait(act, "x1_done", NT)
                    act.activation(sil[:, f, :], bank[2 * f][:], ACT.Silu).then_inc(sem(f"silu{f}"), 1)
                    if f == 0:
                        if down is not None:
                            with act.If(g == down[0]):
                                split_down(down[1], down[0], 2)
                        pieces(g, split, 0, 3)
                        if route:
                            keep_turned(NT)
                if route:
                    wait(act, "x1_out", 16 * NT)
                    wait(act, "x2_out", 16 * NT)
                    wait(act, "x2_turned", NT)
                    wait(act, "logits", NT)
                for f in range(2):
                    wait(act, f"h_turned{f}", g + 1)
                    wait(act, "down_done", g)
                    wait(act, f"hT_l{f}", g)
                    copy(hT["h"][:, 4 * f:4 * f + 4, :], bank[4 + f][:].rearrange("p (c q) -> p c q", c=4)
                         ).then_inc(sem(f"hT_h{f}"), 1)
                    if f == 0:
                        pieces(g, split, 3, 6)
                        if route:
                            router_exp(NT)
                            pick_exp(NT)
                turned_rows(g + 1)
                wait(act, "meta_next", g + 2)
                act.dma_start(e_x[:], rows(source, row)).then_inc(sem("e_x_in"), 16)
                wait(act, "down_done", g + 1)
                wait(act, "meta", g + 1)
                wait(act, "added", g * 16)
                copy(y[:], bank[6][:], scale=meta[:, 0:1]).then_inc(sem("y_done"), 1)
                pieces(g, split, 6, SPLIT_GU)

            split_down(0, 0)
            expert_tile(0, tokens, 2, None, True)
            with act.Fori(1, FIRST - 2) as g:
                expert_tile(g, tokens, g + 2)
            for k in range(4):
                act.wait_ge(sem(f"sent{k}"), NT // 2 * 16)
            act.wait_ge(sem("last_in_slots"), 16)
            assert EARLY == FIRST - 2
            expert_tile(FIRST - 2, slots, 0, (None, 1, 1))
            expert_tile(FIRST - 1, slots, 1)
            act.wait_ge(sem("table"), 1)

            def stage(e, k, split):
                first = act.value_load(table[0:1, bass.ds(e + 1, 1)], min_val=FIRST, max_val=MAX_TILES)
                end = act.value_load(table[0:1, bass.ds(e + 2, 1)], min_val=FIRST, max_val=MAX_TILES)
                if split:
                    when = act.value_load(table[0:1, bass.ds(e + 16, 1)], min_val=0, max_val=MAX_TILES)
                split_down(e + 1, first, 0, 2)
                with act.Fori(first, end) as g:
                    expert_tile(g, slots, g + 2 - FIRST, split and (when, *split), down=(first, e + 1))

            with act.Fori(0, E // 2) as j:
                for k in range(2):
                    stage(2 * j + k, k, (k, j + 1 + k))
            stage(E, 0, None)

        @block.vector
        def _(dve):
            def minus(o, a, b):
                return dve.tensor_tensor(o, a, b.bitcast(F32), ALU.subtract)

            def statistics(a, n, b):
                dve.bn_stats(stat[:], a).then_inc(sem("stat"), 1)
                wait_apart(dve, "stat", n)
                dve.bn_aggr(mv[:, b, :], stat[:]).then_inc(sem("mean_var"), 1)
                wait(dve, "mean_var", n)
                dve.tensor_scalar(var_e[:, b:b + 1], mv[:, b, 1:2], LN_EPS, None, ALU.add).then_inc(sem("var"), 1)

            def normalise(o, a, n, b):
                wait(dve, "rstd", n)
                return dve.tensor_scalar(o, a, mv[:, b, 0:1], rstd[:, b:b + 1], ALU.subtract, ALU.mult)

            def measure(t, b, j):
                dve.wait_ge(sem(f"x_in{b}"), j * 16 + 16)
                wait(dve, "ln1_done", t - 1)
                statistics(x_t[:, b, :], t + 1, b)

            def layer_norm(t, b):
                wait(dve, "xn_turned", t - 1)
                normalise(xn[:, b, :], x_t[:, b, :], t + 1, b).then_inc(sem("ln1_done"), 1)

            dve.wait_ge(sem("consts"), 6)
            dve.wait_ge(sem("in_b"), 32)
            dve.tensor_copy(before_r[:], before[:]).then_inc(sem("triangle"), 1)
            dve.tensor_copy(ones_r[:], ones[:]).then_inc(sem("triangle"), 1)
            for c in range(DC):
                dve.tensor_scalar(bk_rep[:, c, :], ones[:], bqk[:, 1, c:c + 1], None, ALU.mult).then_inc(sem("bk_rep"), 1)
            dve.wait_ge(sem("wqk_h"), 1)
            minus(wq["l"][:], wq_raw[:], wq["h"][:]).then_inc(sem("wqk_l"), 1)
            dve.wait_ge(sem("wqk_h"), 2)
            minus(wk["l"][:], wk_raw[:], wk["h"][:]).then_inc(sem("wqk_l"), 1)
            dve.wait_ge(sem("c2_ps"), 1)
            dve.tensor_copy(c2_rep[:], bank[6][:]).then_inc(sem("c2_done"), 1)
            for c in range(DC):
                dve.wait_ge(sem("wvT_h"), c + 1)
                minus(wvT["l"][:, c, :], bank[c][:], wvT["h"][:, c, :]).then_inc(sem("wvT_l"), 1)

            def A_chunks(m, n):
                for c in range(m, n):
                    dve.wait_ge(sem("A_h"), c + 1)
                    minus(A["l"][:, c, :], bank[4 + c][:], A["h"][:, c, :]).then_inc(sem("A_done"), 1)

            measure(0, 0, 0)
            measure(1, 1, 0)
            layer_norm(0, 0)
            A_chunks(0, 2)
            dve.wait_ge(sem("c2_done"), 1)

            def keep_bias(t):
                wait(dve, "sq_sum", t + 1)
                dve.tensor_copy(s_q[:, bass.ds(t, 1)], tsum[:]).then_inc(sem("sq_done"), 1)

            def before_attention(t, b, this, prev, j, further=True):
                if this:
                    wait(dve, "xT1_h", t + 1)
                    wait(dve, "xnT_l", t - 1)
                    wait(dve, "v_ps", t - 1)
                    minus(xT1["l"][:, b, :, :], bank[b][:].rearrange("p (c q) -> p c q", c=DC),
                          xT1["h"][:, b, :, :]).then_inc(sem("xT1_l"), 1)
                if prev:
                    keep_bias(t - 1)
                if this and (further or b == 0):
                    layer_norm(t + 1, 1 - b)
                if this:
                    wait(dve, "sq_done", t)
                    wait_apart(dve, "ln1_done", t + 1)
                    dve.tensor_tensor_reduce(out=spent[:], in0=xn[:, b, :], in1=c2_rep[:], scale=1.0, scalar=0.0,
                                             op0=ALU.mult, op1=ALU.add, accum_out=tsum[:]).then_inc(sem("sq_sum"), 1)
                if prev:
                    wait(dve, "v_h", t)
                    minus(v["l"][:, bass.ds(t - 1, 1), :], bank[3 - b][:].rearrange("p (a n) -> p a n", a=1),
                          v["h"][:, bass.ds(t - 1, 1), :]).then_inc(sem("v_l"), 1)
                if further:
                    measure(t + 2, b, j + 1)

            before_attention(0, 0, True, False, 0)
            A_chunks(2, DC)
            before_attention(1, 1, True, True, 0)
            before_attention(2, 0, True, True, 1)
            before_attention(3, 1, True, True, 1)
            with dve.Fori(2, NT // 2 - 1) as j:
                before_attention(2 * j, 0, True, True, j)
                before_attention(2 * j + 1, 1, True, True, j)
            before_attention(NT - 2, 0, True, True, NT // 2 - 1, False)
            before_attention(NT - 1, 1, True, True, NT // 2 - 1, False)
            dve.wait_ge(sem("biases"), 1)
            dve.tensor_copy(c1[:], bank[4][:, 0:2 * DC].rearrange("p (c a) -> p c a", a=2)[:, :, 0]).then_inc(sem("c1_done"), 1)
            dve.tensor_copy(bb[:], bank[4][:, 2 * DC:2 * DC + 1]).then_inc(sem("c1_done"), 1)

            def scaled_queries(n, half):
                wait(dve, "y_ps", n + 1)
                wait(dve, "yT_h", n)
                wait(dve, "yT_l", n)
                for c in range(2):
                    m = 2 * half + c
                    ins = dve.tensor_scalar(y_f[:, c, :], bank[7][:, c * 256:(c + 1) * 256], c1[:, m:m + 1], SCALE,
                                            ALU.add, ALU.mult)
                ins.then_inc(sem("yT_f"), 1)

            dve.wait_ge(sem("sq_sum"), NT)
            dve.wait_ge(sem("c1_done"), 2)
            scaled_queries(0, 0)
            before_attention(NT, 0, False, True, NT // 2, False)
            dve.wait_ge(sem("sq_done"), NT)
            dve.wait_ge(sem("c1_done"), 2)
            dve.tensor_scalar(s_q[:], s_q[:], bb[:, 0:1], SCALE, ALU.add, ALU.mult).then_inc(sem("sq_done"), 1)
            dve.wait_ge(sem("sq_done"), NT + 1)

            def pieces(g, split, n, m):
                if split is None:
                    return
                when, s, stage = split
                if when is not None:
                    with dve.If(g == when):
                        pieces(g, (None, s, stage), n, m)
                    return
                for k in range(n, m):
                    wait(dve, "gu_h", stage * SPLIT_GU + k + 1)
                    raw = gate_s_raw if isinstance(stage, int) and stage == 0 and k < DC else gu_raw[s][k // DC]
                    minus(gu_l[s][k // DC][:, k % DC, :], raw[:, k % DC, :],
                          gu_h[s][k // DC][:, k % DC, :]).then_inc(sem("gu_l"), 1)

            def turned_rows(g):
                wait(dve, "e_x_in", g * 16 + 16)
                wait(dve, "meta", g)
                dve.tensor_copy(meta_next[:].bitcast(I32), e_x[:, D:ROW].bitcast(I32)).then_inc(sem("meta_next"), 1)
                wait(dve, "e_xT_h", g + 1)
                minus(e_xT["l"][:], bank[7][:].rearrange("p (c q) -> p c q", c=DC), e_xT["h"][:]).then_inc(sem("e_xT_l"), 1)

            def queries(n, half):
                scaled_queries(n, half)
                queries_low(n, half)

            def queries_low(n, half):
                wait(dve, "yT_h", n + 1)
                minus(yT["l"][:, 2 * half:2 * half + 2, :], y_f[:], yT["h"][:, 2 * half:2 * half + 2, :]).then_inc(sem("yT_l"), 1)

            def mask(i, b, n):
                wait(dve, "scores", 4 * i + n + 1)
                if n == 0:
                    wait(dve, "adj_in", i * 16 + 16)
                    wait(dve, "p_turned", 4 * (i - 1))
                dve.scalar_tensor_tensor(out=sc[:, b, n * 512:(n + 1) * 512], in0=bank[n][:], scalar=s_q[:, bass.ds(i, 1)],
                                         in1=adj_t[:, n * 512:(n + 1) * 512], op0=ALU.add, op1=ALU.mult
                                         ).then_inc(sem("scored"), 1)

            def fill_zeros(i, b, n):
                part = sc[:, b, n * 512:(n + 1) * 512]
                wait(dve, "scored", 4 * i + n + 1)
                wait(dve, "filled", 4 * i + n)
                dve.tensor_scalar(fill[:], part, 0.0, MASKED, ALU.is_equal, ALU.mult).then_inc(sem("zeros"), 1)
                if n == 0:
                    wait(dve, "nmx_done", i)
                wait_apart(dve, "zeros", 4 * i + n + 1)
                dve.tensor_tensor_reduce(out=part, in0=part, in1=fill[:], scale=1.0, scalar=-3.0e38, op0=ALU.add,
                                         op1=ALU.max, accum_out=mx4[:, n:n + 1]).then_inc(sem("filled"), 1)

            def row_max(i, b):
                wait(dve, "filled", 4 * i + 4)
                wait(dve, "exp_done", i - 1)
                dve.tensor_reduce(nmx[:, b:b + 1], mx4[:], AX, ALU.max, negate=True).then_inc(sem("nmx_done"), 1)

            def group(i, g):
                n = 4 * i + g
                wait(dve, "pT_h", n + 1)
                minus(pT["l"][:, g % 2, :], bank[4 + g % 2][:], pT["h"][:, g % 2, :]).then_inc(sem("pT_l"), 1)

            def output(i, b):
                wait(dve, "exp_done", i)
                wait(dve, "o_done", i - 1)
                dve.reciprocal(rden[:], den[:, 1 - b:2 - b]).then_inc(sem("rden_done"), 1)
                wait(dve, "attended", 4 * i)
                wait(dve, "x1_out", 16 * (i - 1))
                wait(dve, "x2_done", i - 1)
                wait(dve, "rden_done", i)
                dve.scalar_tensor_tensor(out=x1[:], in0=bank[6][:], scalar=rden[:, 0:1], in1=bv_row[:], op0=ALU.mult,
                                         op1=ALU.add).then_inc(sem("o_done"), 1)

            def residual(i, b, n):
                dve.wait_ge(sem(f"xr_in{1 - b}"), n * 16)
                wait(dve, "o_done", i)
                dve.scalar_tensor_tensor(out=x1[:], in0=x1[:], scalar=0.0, in1=x_t[:, 1 - b, :], op0=ALU.max,
                                         op1=ALU.add).then_inc(sem("x1_done"), 1)
                wait(dve, "x1_done", i)
                statistics(x1[:], NT + i, 1 - b)
                wait(dve, "x2_out", 16 * (i - 1))
                wait(dve, "x2_turned", i - 1)
                normalise(x2row[:, 0:D], x1[:], NT + i, 1 - b).then_inc(sem("x2_done"), 1)

            ROUTER = 15

            def logits(i):
                wait(dve, "logits", i)
                dve.tensor_copy(lg[:], bank[7][:, 0:E]).then_inc(sem("logits_read"), 1)
                wait(dve, "logits_read", i)
                dve.tensor_reduce(nlm[:], lg[:], AX, ALU.max, negate=True).then_inc(sem("nlm_done"), 1)

            steps = [0]

            def then_route(i, ins):
                steps[0] += 1
                ins.then_inc(sem("routing"), 1)
                wait_apart(dve, "routing", (i - 1) * ROUTER + steps[0])

            def picks(i):
                steps[0] = 0
                wait(dve, "lex_done", i)
                then_route(i, dve.reciprocal(lrs[:], lsum[:]))
                then_route(i, dve.tensor_scalar(rw[:], lex[:], lrs[:, 0:1], None, ALU.mult))
                then_route(i, dve.max(top[:], rw[:]))
                then_route(i, dve.max_index(topi[:], top[:], rw[:]))
                dve.tensor_tensor(tdiff[:], top[:, 1:2], top[:, 0:1], ALU.subtract).then_inc(sem("tdiff_done"), 1)
                then_route(i, dve.tensor_copy(topf[:], topi[:, 0:2]))
                for k in range(2):
                    then_route(i, dve.tensor_scalar(route[:, k * E:(k + 1) * E], iota8[:], topf[:, k:k + 1], None, ALU.is_equal))
                dve.tensor_tensor(both[:], route[:, 0:E], route[:, E:2 * E], ALU.add).then_inc(sem("picked"), 1)

            def pick_weights(i):
                wait(dve, "tex_done", i)
                then_route(i, dve.tensor_scalar(tsum[:], tex[:], 1.0, None, ALU.add))
                then_route(i, dve.reciprocal(route[:, 2 * E + 2:2 * E + 3], tsum[:]))
                then_route(i, dve.tensor_tensor(route[:, 2 * E + 3:2 * E + 4], tex[:], route[:, 2 * E + 2:2 * E + 3], ALU.mult))

            def take_counts(i):
                wait(dve, "counted", i)
                dve.tensor_copy(counts[:], bank[7][:, 0:2 * E]).then_inc(sem("counts_read"), 1)

            def ranks(i):
                steps[0] = ROUTER - 5
                wait(dve, "counts_read", i)
                then_route(i, dve.tensor_tensor(rank[:], counts[:, 0:E], base[:], ALU.add))
                for k in range(2):
                    then_route(i, dve.tensor_tensor_reduce(out=rsel[:], in0=route[:, k * E:(k + 1) * E], in1=rank[:], scale=1.0,
                                                           scalar=0.0, op0=ALU.mult, op1=ALU.add,
                                                           accum_out=route[:, 2 * E + k:2 * E + k + 1]))
                then_route(i, dve.tensor_copy(routes[:, bass.ds(i - 1, 1), :], route[:].rearrange("p (a n) -> p a n", a=1)))
                then_route(i, dve.tensor_tensor(base[:], base[:], counts[:, E:2 * E], ALU.add))
                assert steps[0] == ROUTER

            def attention_step(j, b, last=False, prev=True, split=False):
                i = 2 * j + b
                if prev:
                    output(i, b)
                if last:
                    group(i, 0)
                    group(i, 1)
                    residual(i, b, j + b)
                    pieces(0, (None, 0, 0), 2, 3)
                    group(i, 2)
                    ranks(i - 1)
                    pieces(0, (None, 0, 0), 3, 4)
                    logits(i)
                    group(i, 3)
                    picks(i)
                    pick_weights(i)
                    pieces(0, (None, 0, 0), 4, 5)
                    take_counts(i)
                    pieces(0, (None, 0, 0), 5, 6)
                    return
                if prev:
                    residual(i, b, j + b)
                mask(i + 1, 1 - b, 0)
                mask(i + 1, 1 - b, 1)
                group(i, 0)
                group(i, 1)
                fill_zeros(i + 1, 1 - b, 0)
                fill_zeros(i + 1, 1 - b, 1)
                mask(i + 1, 1 - b, 2)
                if prev:
                    logits(i)
                fill_zeros(i + 1, 1 - b, 2)
                if prev and not (isinstance(i, int) and i == 1):
                    ranks(i - 1)
                mask(i + 1, 1 - b, 3)
                fill_zeros(i + 1, 1 - b, 3)
                ahead = queries_follow(j, b)
                if ahead:
                    queries(2 * j + 2, 0)
                group(i, 2)
                if prev:
                    picks(i)
                    pick_weights(i)
                if ahead:
                    queries(2 * j + 3, 1)
                group(i, 3)
                row_max(i + 1, 1 - b)
                if split:
                    pieces(0, (None, 0, 0), 0, 2)
                if prev:
                    take_counts(i)

            queries_low(0, 0)
            queries(1, 1)
            for n in range(KB):
                mask(0, 0, n)
                fill_zeros(0, 0, n)
            row_max(0, 0)
            dve.wait_ge(sem("in_bv"), 16)
            attention_step(0, 0, prev=False)
            attention_step(0, 1)
            with dve.Fori(1, NT // 2 - 1) as j:
                attention_step(j, 0)
                attention_step(j, 1)
            attention_step(NT // 2 - 1, 0, split=True)
            attention_step(NT // 2 - 1, 1, last=True)
            turned_rows(0)
            pieces(0, (None, 0, 0), 6, SPLIT_GU)
            output(NT, 0)
            residual(NT, 0, NT // 2)
            ranks(NT - 1)

            def split_down(stage, m=0, n=SPLIT_DN):
                for c in range(m, n):
                    k = FC // SPLIT_DN
                    wait(dve, "dn_h", stage * SPLIT_DN + c + 1)
                    minus(dn_l[:, c * k:(c + 1) * k, :], dn_raw[:, c * k:(c + 1) * k, :],
                          dn_h[:, c * k:(c + 1) * k, :]).then_inc(sem("dn_l"), 1)

            def expert_tile(g, split=None, route=False, down=None):
                for f in range(2):
                    if route and f == 1:
                        logits(NT)
                    wait(dve, f"silu{f}", g + 1)
                    wait(dve, "up0" if f == 0 else "up_done", g + 1)
                    wait(dve, f"h_turned{f}", g)
                    dve.tensor_tensor(hid[:, f, :], bank[2 * f + 1][:], sil[:, f, :], ALU.mult).then_inc(sem(f"hid{f}"), 1)
                    if f == 0:
                        if route:
                            split_down(0, 2)
                        if down is not None:
                            with dve.If(g == down[0]):
                                split_down(down[1], 2)
                        wait(dve, "added", g * 16)
                        wait(dve, "y_done", g)
                        wait(dve, "meta_next", g + 1)
                        dve.tensor_copy(meta[:].bitcast(I32), meta_next[:].bitcast(I32)).then_inc(sem("meta"), 1)
                        pieces(g, split, 0, 2)
                        hidden(g, 0)
                        pieces(g, split, 2, 3)
                pieces(g, split, 3, 4)
                if route:
                    picks(NT)
                hidden(g, 1)
                if route:
                    take_counts(NT)
                    pick_weights(NT)
                    ranks(NT)
                turned_rows(g + 1)
                pieces(g, split, 4, SPLIT_GU)

            def hidden(g, f):
                wait(dve, f"hT_h{f}", g + 1)
                minus(hT["l"][:, 4 * f:4 * f + 4, :], bank[4 + f][:].rearrange("p (c q) -> p c q", c=4),
                      hT["h"][:, 4 * f:4 * f + 4, :]).then_inc(sem(f"hT_l{f}"), 1)

            chain = [0]

            def then(ins):
                chain[0] += 1
                ins.then_inc(sem("placing"), 1)
                dve.wait_ge(sem("placing"), chain[0])

            def also(ins):
                chain[0] += 1
                ins.then_inc(sem("placing"), 1)

            def place_picks():
                then(dve.tensor_scalar(tiles_f[:], base[:], float(P - 1), None, ALU.add))
                then(dve.tensor_copy(cnt_i[:], tiles_f[:]))
                then(dve.tensor_scalar(tiles_i[:], cnt_i[:], P.bit_length() - 1, None, ALU.arith_shift_right))
                then(dve.tensor_scalar(tiles_f[:], tiles_i[:], 1.0, None, ALU.max))
                then(dve.memset(bnd[:, 0:1], 0.0))
                then(dve.memset(bnd[:, 1:2], float(FIRST)))
                for e in range(E):
                    then(dve.tensor_tensor(bnd[:, e + 2:e + 3], bnd[:, e + 1:e + 2], tiles_f[:, e:e + 1], ALU.add))
                then(dve.tensor_scalar(bnd[:, E + 2:E + 3], bnd[:, E + 1:E + 2], float(LAST), None, ALU.add))
                then(dve.tensor_scalar(cut[:, 0, :], bnd[:, 0:E + 1], 1.0, None, ALU.add))
                then(dve.tensor_scalar(cut[:, 1, :], bnd[:, 1:E + 2], -1.0, None, ALU.add))
                then(dve.tensor_tensor(cut[:, 0, :], cut[:, 0, :], cut[:, 1, :], ALU.min))
                then(dve.tensor_copy(table[:, 0:E + 3], bnd[:]))
                then(dve.tensor_copy(table[:, 16:16 + E], cut[:, 0, 1:E + 1]))
                then(dve.tensor_scalar(off[:], bnd[:, 1:E + 1], float(P), -float(P * FIRST), ALU.mult, ALU.add))
                for k in range(2):
                    for e in range(E):
                        (then if e == E - 1 else also)(dve.tensor_scalar(place[:, :, e], routes[:, :, k * E + e], off[:, e:e + 1], None, ALU.mult))
                    then(dve.tensor_reduce(where[:], place[:], AX, ALU.add))
                    then(dve.tensor_tensor(wherek[:], where[:], routes[:, :, 2 * E + k], ALU.add))
                    then(dve.tensor_copy(pos_i[:, k, :], wherek[:]))
                dve.tensor_copy(bnd[:, 0:1], bnd[:, 0:1]).then_inc(sem("table"), 1)

            split_down(0, 0, 2)
            for g in range(UNPLACED):
                expert_tile(g, None, g == 0)
            place_picks()
            with dve.Fori(UNPLACED, EARLY) as g:
                expert_tile(g)
            expert_tile(EARLY, (None, 1, 1))
            expert_tile(FIRST - 1)

            def stage(e, split):
                first = dve.value_load(table[0:1, bass.ds(e + 1, 1)], min_val=FIRST, max_val=MAX_TILES)
                end = dve.value_load(table[0:1, bass.ds(e + 2, 1)], min_val=FIRST, max_val=MAX_TILES)
                if split:
                    when = dve.value_load(table[0:1, bass.ds(e + 16, 1)], min_val=0, max_val=MAX_TILES)
                split_down(e + 1, 0, 2)
                with dve.Fori(first, end) as g:
                    expert_tile(g, split and (when, *split), down=(first, e + 1))

            with dve.Fori(0, E // 2) as j:
                for k in range(2):
                    stage(2 * j + k, (k, 2 * j + k + 2))
            stage(E, None)


_INS = ['x', 'adj', 'L0_gnn_W_q', 'L0_gnn_b_q', 'L0_gnn_W_k', 'L0_gnn_b_k', 'L0_gnn_W_v', 'L0_gnn_b_v',
        'L0_ffn_Wr', 'L0_ffn_Wg_s', 'L0_ffn_Wu_s', 'L0_ffn_Wd_s', 'L0_ffn_Wg', 'L0_ffn_Wu', 'L0_ffn_Wd']
_OUTS = [((2048, 512), 'float32')]


def kernel(**inputs):
    import numpy as _np
    import concourse.bacc as _bacc
    from concourse import mybir as _mybir
    from concourse.bass_utils import run_bass_kernel_spmd as _run

    nc = _bacc.Bacc("TRN2", target_bir_lowering=False, num_devices=1)
    arrays, args = {}, []
    for name in _INS:
        a = _np.ascontiguousarray(inputs[name])
        arrays[f"in_{name}_dram"] = a
        args.append(nc.dram_tensor(f"in_{name}_dram", a.shape, _mybir.dt.from_np(a.dtype), kind="ExternalInput").ap())
    for i, (shape, dtype) in enumerate(_OUTS):
        dt = _mybir.dt.from_np(_np.dtype(dtype))
        args.append(nc.dram_tensor(f"out_{i}_dram", shape, dt, kind="ExternalOutput").ap())
    gnn_moe(nc, *args)
    r = _run(nc, [arrays], core_ids=[0])
    got = tuple(r.results[0][f"out_{i}_dram"] for i in range(len(_OUTS)))
    return got[0]
```
